# Optimizing a Trainium2 kernel written in Bass

```python
import numpy as np
import jax
import jax.numpy as jnp

def _softmax(x, axis=-1):
    return jax.nn.softmax(x, axis=axis)

def _gelu(x):
    return jax.nn.gelu(x, approximate=True)

def _silu(x):
    return jax.nn.silu(x)

def _sigmoid(x):
    return jax.nn.sigmoid(x)

def _layernorm(x, axis=-1, eps=1e-05):
    m = jnp.mean(x, axis=axis, keepdims=True)
    v = jnp.var(x, axis=axis, keepdims=True)
    return (x - m) / jnp.sqrt(v + eps)

def _scatter_add(tgt, idx, src, axis=0):
    return tgt.at[idx].add(src)

def _segment_sum(src, seg, n):
    return jax.ops.segment_sum(src, seg, n)
kernel_name = 'mk_gnn_resnorm_d2_gnn_r64_50d296'

def setup_inputs(seed: int=0):
    np.random.seed(seed)
    _w = jnp.asarray

    def _rec_inputs():
        import jax
        import jax.numpy as jnp
        _gk = jax.random.key(seed)
        x = -0.000202 + 1 * jax.random.normal(jax.random.fold_in(_gk, 1), (100000, 128), jnp.float32)
        src = jax.random.randint(jax.random.fold_in(_gk, 2), (50000,), 0, 100000, jnp.int32)
        dst = jnp.minimum((100000 * jax.random.uniform(jax.random.fold_in(_gk, 3), (50000,)) ** 2.0).astype(jnp.int32), 99999)
        _o = jnp.argsort(dst, stable=True)
        src = src[_o]
        dst = dst[_o]
        edge_type_4 = jax.random.randint(jax.random.fold_in(_gk, 12), (50000,), 0, 4, jnp.int32)
        edge_weight = jax.random.uniform(jax.random.fold_in(_gk, 13), (50000,), jnp.float32, 0.0, 0.999996)
        return (x, src, dst, edge_type_4, edge_weight)
    x, src, dst, edge_type_4, edge_weight = _rec_inputs()

    def _L0_gnn_setup():
        import jax, jax.numpy as jnp
        import numpy as np
        key = jax.random.key(seed)
        k1, k2, k3 = jax.random.split(key, 3)
        N, E, D_IN, D_OUT = (50000, 12500, 128, 128)
        x = jax.random.normal(k1, (N, D_IN), dtype=jnp.float32)
        edge_index = jax.random.randint(k2, (2, E), 0, N, dtype=jnp.int64)
        W = jax.random.normal(k3, (D_OUT, D_IN), dtype=jnp.float32) * (1.0 / np.sqrt(D_IN))
        return {'x': x, 'edge_index': edge_index, 'W': W}
    _L0_gnn_all = _L0_gnn_setup()
    _L0_gnn_in = {k: v for k, v in _L0_gnn_all.items() if k in ('W',)}
    del _L0_gnn_all

    def _L1_gnn_setup():
        import jax, jax.numpy as jnp
        import numpy as np
        NUM_RELATIONS = 4
        N_NODES = 20000
        N_EDGES = 5000
        F_IN = 128
        HID = 128
        EMB = 128

        def _rgcn_conv(x, src, dst, edge_type, edge_weight, W, root, bias):
            xj = x[src]
            m = jnp.zeros((xj.shape[0], W.shape[2]), dtype=x.dtype)
            for r in range(W.shape[0]):
                mask = (edge_type == r).astype(x.dtype)[:, None]
                m = m + mask * (xj @ W[r])
            m = m * edge_weight[:, None]
            out = jax.ops.segment_sum(m, dst, num_segments=x.shape[0])
            return out + x @ root + bias
        key = jax.random.key(seed)
        ks = jax.random.split(key, 10)
        return {'x': jax.random.normal(ks[0], (N_NODES, F_IN), dtype=jnp.float32), 'edge_index': jax.random.randint(ks[1], (2, N_EDGES), 0, N_NODES, dtype=jnp.int64 if jax.config.jax_enable_x64 else jnp.int32).astype(jnp.int32), 'edge_type': jax.random.randint(ks[2], (N_EDGES,), 0, NUM_RELATIONS).astype(jnp.int32), 'edge_weight': jax.random.uniform(ks[3], (N_EDGES,), dtype=jnp.float32), 'W1': jax.random.normal(ks[4], (NUM_RELATIONS, F_IN, HID), dtype=jnp.float32) * 0.05, 'root1': jax.random.normal(ks[5], (F_IN, HID), dtype=jnp.float32) * 0.05, 'b1': jax.random.normal(ks[6], (HID,), dtype=jnp.float32) * 0.05, 'W2': jax.random.normal(ks[7], (NUM_RELATIONS, HID, EMB), dtype=jnp.float32) * 0.05, 'root2': jax.random.normal(ks[8], (HID, EMB), dtype=jnp.float32) * 0.05, 'b2': jax.random.normal(ks[9], (EMB,), dtype=jnp.float32) * 0.05}
    _L1_gnn_all = _L1_gnn_setup()
    _L1_gnn_in = {k: v for k, v in _L1_gnn_all.items() if k in ('W1', 'root1', 'b1', 'W2', 'root2', 'b2')}
    del _L1_gnn_all
    return {'x': x, 'src': src, 'dst': dst, 'edge_type_4': edge_type_4, 'edge_weight': edge_weight, 'L0_gnn_W': _L0_gnn_in['W'], 'L1_gnn_W1': _L1_gnn_in['W1'], 'L1_gnn_root1': _L1_gnn_in['root1'], 'L1_gnn_b1': _L1_gnn_in['b1'], 'L1_gnn_W2': _L1_gnn_in['W2'], 'L1_gnn_root2': _L1_gnn_in['root2'], 'L1_gnn_b2': _L1_gnn_in['b2']}

def reference(x, src, dst, edge_type_4, edge_weight, L0_gnn_W, L1_gnn_W1, L1_gnn_root1, L1_gnn_b1, L1_gnn_W2, L1_gnn_root2, L1_gnn_b2):
    import jax
    import jax.numpy as jnp

    def _L0_gnn_ref(x, edge_index, W):
        import jax, jax.numpy as jnp
        import numpy as np
        h = x @ W.T
        N = x.shape[0]
        src, dst = (edge_index[0], edge_index[1])
        agg = jax.ops.segment_sum(h[src], dst, num_segments=N)
        return agg + h

    def _L1_gnn_ref(x, edge_index, edge_type, edge_weight, W1, root1, b1, W2, root2, b2):
        import jax, jax.numpy as jnp
        import numpy as np
        NUM_RELATIONS = 4
        N_NODES = 20000
        N_EDGES = 5000
        F_IN = 128
        HID = 128
        EMB = 128

        def _rgcn_conv(x, src, dst, edge_type, edge_weight, W, root, bias):
            xj = x[src]
            m = jnp.zeros((xj.shape[0], W.shape[2]), dtype=x.dtype)
            for r in range(W.shape[0]):
                mask = (edge_type == r).astype(x.dtype)[:, None]
                m = m + mask * (xj @ W[r])
            m = m * edge_weight[:, None]
            out = jax.ops.segment_sum(m, dst, num_segments=x.shape[0])
            return out + x @ root + bias
        src, dst = (edge_index[0], edge_index[1])
        ew = (edge_weight - edge_weight.min()) / (edge_weight.max() - edge_weight.min() + 1e-08)
        h = jax.nn.relu(_rgcn_conv(x, src, dst, edge_type, ew, W1, root1, b1))
        h = _rgcn_conv(h, src, dst, edge_type, ew, W2, root2, b2)
        return h
    edge_index = jnp.stack([src, dst])
    x = _layernorm(x + _L0_gnn_ref(x, edge_index, L0_gnn_W), axis=-1)
    x = _layernorm(x + _L1_gnn_ref(x, edge_index, edge_type_4, edge_weight, L1_gnn_W1, L1_gnn_root1, L1_gnn_b1, L1_gnn_W2, L1_gnn_root2, L1_gnn_b2), axis=-1)
    return x

_drawn_inputs = setup_inputs


def setup_inputs(seed=0):
    import zlib

    import numpy as np

    out = dict(_drawn_inputs(seed))
    spreads = {}
    factors = {'L1_gnn_b1': 2.747}
    for name, (base, spread) in spreads.items():
        noise = np.random.default_rng([zlib.crc32(name.encode()), seed]).standard_normal(out[name].shape)
        drawn = base * np.exp(spread * noise) if base else spread * noise
        out[name] = jnp.asarray(drawn.astype(out[name].dtype))
    for name, factor in factors.items():
        out[name] = (out[name] * factor).astype(out[name].dtype)
    return out
```

```python
from contextlib import ExitStack, contextmanager

import concourse.bass as bass
from concourse import mybir

FP32 = mybir.dt.float32
BF16 = mybir.dt.bfloat16
I32 = mybir.dt.int32
ALU = mybir.AluOpType
ACT = mybir.ActivationFunctionType
AX = mybir.AxisListType

P = 128
TPB = 4
UNROLL = 4
PAIRS = 2
CPB = 4
CPH = CPB // 2
WIDE = 2 * P
BLOCK = CPB * P
RING = 4
RELATIONS = 4
ROW = P + 4
DIGIT = 32
NO_NODE = float(1 << 20)
LN_EPS = 1e-5
EW_EPS = 1e-8


class Shapes:

    def __init__(self, nodes, edges):
        self.nodes, self.edges = nodes, edges
        self.batches = -(-nodes // (P * TPB * UNROLL)) * UNROLL
        self.tiles = self.batches * TPB
        self.tail = nodes - (self.batches - 1) * TPB * P
        assert 0 < self.tail <= TPB * P and self.tiles < DIGIT * DIGIT
        self.blocks = -(-(edges + WIDE) // BLOCK)
        assert self.blocks <= P
        self.first_row = WIDE
        self.rows = WIDE + (self.blocks + 1) * BLOCK


class At:

    def __init__(self, b, slot, turn):
        self.b, self.slot, self.turn = b, slot, turn

    def back(self, n):
        return At(self.b - n, (self.slot - n) % 4, self.turn - (1 if self.slot < n else 0))

    def ahead(self, n):
        return At(self.b + n, (self.slot + n) % 4, self.turn + (1 if self.slot + n >= 4 else 0))

    def within(self, count):
        return not isinstance(self.b, int) or 0 <= self.b < count

    def at_least(self, n):
        return not isinstance(self.b, int) or self.b >= n


def each(engine, body, count, drain=0):
    turns = (count - 1) // 4
    for b in range(min(4, count)):
        body(At(b, b, 0))
    if turns > 1:
        with engine.Fori(1, turns) as turn:
            for slot in range(4):
                body(At(turn * 4 + slot, slot, turn))
    for b in range(4 * turns if turns > 1 else 4, count + drain):
        body(At(b, b % 4, b // 4))


@contextmanager
def phase_semaphores(nc, prefix=""):
    used = []
    with ExitStack() as ctx:
        def sem(name):
            used.append(ctx.enter_context(nc.semaphore(prefix + name)))
            return used[-1]

        yield sem
        with nc.Block() as block:
            @block.gpsimd
            def _(pool):
                for each_used in used:
                    pool.sem_clear(each_used)


def setup_phase(nc, s, k, dram):
    NB = s.blocks
    full = s.edges // BLOCK
    rest = s.edges - full * BLOCK
    with ExitStack() as ctx:
        sb = lambda n, sh, dt=FP32: ctx.enter_context(nc.sbuf_tensor(n, sh, dt))
        sem = ctx.enter_context(phase_semaphores(nc))
        raw_i = [sb(f"raw_{n}", [NB, BLOCK], I32) for n in ("dst", "src", "type")]
        raw_f = [sb(f"rawf_{n}", [NB, BLOCK]) for n in ("dst", "src", "type", "weight")]
        next_i = sb("next_dst_i", [NB, BLOCK], I32)
        next_f = sb("next_dst", [NB, BLOCK])
        descents = sb("descents", [P, 1])
        raw_m = sb("raw_w0", [P, P])
        type_col = sb("type_col", [P, NB * CPB])
        w_col = sb("w_col", [P, NB * CPB])
        extremes = sb("extremes", [P, 2])
        ext_t = sb("ext_t", [2, 1])
        ext_d = sb("ext_d", [2, 2])
        ext_b = sb("ext_b", [P, 2])
        span = sb("span", [P, 2])
        ones = sb("ones_setup", [P, P])
        dst_int = sb("dst_int", [P, NB * CPB], I32)
        digit_i = [sb(f"digit_i{i}", [P, NB * CPB], I32) for i in range(2)]
        digit_f = [sb(f"digit_f{i}", [P, NB * CPB]) for i in range(2)]
        hot = [sb(f"digit_hot{i}", [P, NB * CPB, DIGIT], BF16) for i in range(2)]
        counts = sb("counts", [DIGIT, DIGIT])
        running = sb("running", [DIGIT, DIGIT])
        below = sb("below", [DIGIT, DIGIT])
        zeros_d = sb("zeros_digit", [DIGIT, DIGIT])
        starts = sb("starts", [DIGIT, DIGIT])
        row = sb("start_row", [1, DIGIT * DIGIT])
        size = sb("pair_size", [1, s.batches, PAIRS])
        crowd = sb("crowded", [1, s.batches])
        wide = sb("wide", [1, s.batches])
        calm = sb("calm", [1, s.batches])
        flag = sb("unsorted_flag", [1, 2])
        scratch = sb("table_scratch", [1, s.batches])
        scratch_i = sb("table_scratch_i", [1, s.batches], I32)
        need_i = sb("need_i", [1, s.batches], I32)
        need_f = sb("need_f", [1, s.batches])
        pads = sb("pad_rows", [P, CPB * ROW])
        bias_f = [sb(f"bias_f{i}", [3, P]) for i in range(2)]
        part = [[sb(f"part{i}{j}", [3, P], BF16) for j in range(3)] for i in range(2)]
        left = [[sb(f"left{i}{j}", [3, P]) for j in range(2)] for i in range(2)]
        pick = [[sb(f"pick{i}{j}", [3, P]) for j in range(2)] for i in range(2)]
        tp = ctx.enter_context(nc.psum_tensor("tp_setup", [P, 4, CPB * P], FP32))
        small = ctx.enter_context(nc.psum_tensor("small_setup", [P, 4, CPB * P], FP32))
        loaded = sem("edges_loaded")
        padded = sem("padding_written")
        consts = sem("constants_made")
        dve_step = sem("setup_vector_step")
        floats_ready = sem("floats_ready")
        turned = sem("edges_transposed")
        extremes_ready = sem("extremes_ready")
        extremes_turned = sem("extremes_transposed")
        diagonal_ready = sem("diagonal_ready")
        extremes_spread = sem("extremes_spread")
        hot_ready = sem("digits_ready")
        counted = sem("tiles_counted")
        running_ready = sem("running_ready")
        offsets_done = sem("offsets_done")
        starts_ready = sem("starts_ready")
        descents_ready = sem("descents_ready")
        descents_summed = sem("descents_summed")
        row_loaded = sem("start_row_loaded")
        pads_ready = sem("pads_ready")
        pads_stored = sem("pads_stored")

        loads = []
        arrays = (dram.dst, dram.src, dram.type, dram.w)
        blocks_of = lambda a, lo, n: a[lo:lo + BLOCK * n].rearrange("(b e) -> b e", e=BLOCK)
        line = lambda a, lo, hi: a[lo:hi].rearrange("(o e) -> o e", o=1)
        for n, (buf, arr) in enumerate(zip(raw_i + [raw_f[3]], arrays)):
            loads.append((buf[0:full, :], blocks_of(arr, 0, full)))
            if rest:
                loads.append((buf[full:full + 1, 0:rest], line(arr, full * BLOCK, s.edges)))
            if n:
                if rest:
                    loads.append((buf[full:full + 1, rest:BLOCK], line(arr, 0, BLOCK - rest)))
                done = full + (1 if rest else 0)
                if done < NB:
                    loads.append((buf[done:NB, :], blocks_of(arr, 0, NB - done)))
        after_full = (s.edges - 1) // BLOCK
        after_rest = s.edges - 1 - after_full * BLOCK
        loads.append((next_i[0:after_full, :], blocks_of(dram.dst, 1, after_full)))
        if after_rest:
            loads.append((next_i[after_full:after_full + 1, 0:after_rest],
                          line(dram.dst, 1 + after_full * BLOCK, s.edges)))
        for r, root in enumerate((dram.root1, dram.root2)):
            loads.append((k.root[r][:], root))
        for r, w in enumerate((dram.w1, dram.w2)):
            loads.append((k.wrel[r][:].rearrange("p (r n) -> p r n", r=RELATIONS), w.rearrange("r p n -> p r n")))
        loads.append((raw_m[:], dram.w0))
        for r, b in enumerate((dram.b1, dram.b2)):
            loads.append((bias_f[r][:], b.rearrange("(o n) -> o n", o=1).to_broadcast([3, P])))

        block = ctx.enter_context(nc.Block())

        @block.sync
        def _(sp):
            sp.wait_ge(padded, 2)
            for out, in_ in loads:
                sp.dma_start(out, in_).then_inc(loaded, 16)
            sp.wait_ge(pads_ready, 1)
            sp.dma_start(dram.edge_rows[0:WIDE, :].rearrange("(p c) r -> p (c r)", c=WIDE // P),
                         pads[:, 0:WIDE // P * ROW]).then_inc(pads_stored, 16)
            last = s.first_row + s.blocks * BLOCK
            sp.dma_start(dram.edge_rows[last:last + BLOCK, :].rearrange("(p c) r -> p (c r)", c=CPB),
                         pads[:]).then_inc(pads_stored, 16)
            sp.wait_ge(starts_ready, 1)
            sp.dma_start(dram.starts.rearrange("o (a b) -> (o a) b", b=DIGIT), starts[:]).then_inc(row_loaded, 16)
            sp.wait_ge(row_loaded, 16)
            sp.dma_start(row[:], dram.starts).then_inc(row_loaded, 16)
            sp.wait_ge(row_loaded, 32)
            sp.wait_ge(pads_stored, 32)

        @block.gpsimd
        def _(pool):
            nc.gpsimd.memset(ones[:], 1.0).then_inc(consts, 1)
            nc.gpsimd.iota(k.node[:], pattern=[[1, TPB * P]], base=0, channel_multiplier=0,
                           allow_small_or_imprecise_dtypes=True).then_inc(consts, 1)
            nc.gpsimd.iota(k.base[:], pattern=[[TPB * P, s.batches]], base=0, channel_multiplier=0,
                           allow_small_or_imprecise_dtypes=True).then_inc(consts, 1)
            pool.wait_ge(consts, 3)
            nc.gpsimd.affine_select(out=k.ident[:], in_=ones[:], compare_op=ALU.is_equal, fill=0.0,
                                    base=0, pattern=[[-1, P]], channel_multiplier=1).then_inc(consts, 1)
            nc.gpsimd.affine_select(out=below[:], in_=ones[0:DIGIT, 0:DIGIT], compare_op=ALU.is_gt, fill=0.0,
                                    base=0, pattern=[[1, DIGIT]], channel_multiplier=-1).then_inc(consts, 1)

        @block.vector
        def _(dve):
            v = nc.vector
            made = [0]

            def link(ins, ready=None):
                made[0] += 1
                ins.then_inc(dve_step, 1)
                dve.wait_ge(dve_step, made[0])
                if ready is not None:
                    dve.sem_inc(ready, 1)

            v.memset(raw_i[0][:], int(NO_NODE)).then_inc(padded, 1)
            v.memset(next_i[:], int(NO_NODE)).then_inc(padded, 1)
            link(v.memset(k.zeros[:], 0.0))
            link(v.memset(k.ones3[:], 1.0))
            link(v.memset(zeros_d[:], 0.0))
            link(v.memset(pads[:], 0.0))
            pad_dst = pads[:].rearrange("p (c r) -> p c r", r=ROW)[:, :, P:P + 1]
            link(v.memset(pad_dst, NO_NODE), pads_ready)
            dve.wait_ge(consts, 5)
            dve.wait_ge(loaded, 16 * len(loads))
            for n in range(3):
                link(v.tensor_copy(raw_f[n][:], raw_i[n][:]), floats_ready if n == 2 else None)
            link(v.tensor_copy(next_f[:], next_i[:]))
            link(v.tensor_tensor(next_f[:], next_f[:], raw_f[0][:], ALU.is_lt))
            link(v.memset(descents[:], 0.0))
            link(v.tensor_reduce(descents[0:NB, :], next_f[:], AX.X, ALU.add), descents_ready)
            col = lambda t: t[:].rearrange("p (b c) -> p c b", c=CPB)
            dve.wait_ge(turned, 1)
            for n, out in enumerate((k.dst_col, k.src_col, type_col, w_col)):
                link(v.tensor_copy(col(out), tp[:, n].rearrange("p (c b) -> p c b", c=CPB)[:, :, 0:NB]))
            link(v.tensor_reduce(extremes[:, 0:1], w_col[:], AX.X, ALU.max))
            link(v.tensor_reduce(extremes[:, 1:2], w_col[:], AX.X, ALU.min))
            link(v.tensor_scalar(extremes[:, 1:2], extremes[:, 1:2], -1.0, None, ALU.mult), extremes_ready)
            dve.wait_ge(extremes_turned, 1)
            link(v.tensor_reduce(ext_t[:], small[0:2, 0, 0:P], AX.X, ALU.max))
            link(v.tensor_scalar(ext_d[:], k.ident[0:2, 0:2], ext_t[:, 0:1], None, ALU.mult), diagonal_ready)
            link(v.tensor_copy(k.w0t[:], small[:, 1, 0:P]))
            dve.wait_ge(extremes_spread, 1)
            link(v.tensor_copy(ext_b[:], small[:, 2, 0:2]))
            link(v.tensor_scalar(span[:, 0:1], ext_b[:, 0:1], ext_b[:, 1:2], EW_EPS, ALU.add, ALU.add))
            link(v.reciprocal(span[:, 1:2], span[:, 0:1]))
            link(v.tensor_scalar(w_col[:], w_col[:], ext_b[:, 1:2], span[:, 1:2], ALU.add, ALU.mult))
            coef = k.coef[:].rearrange("p (q r) -> p q r", r=RELATIONS)
            for r in range(RELATIONS):
                link(v.scalar_tensor_tensor(out=coef[:, :, r], in0=type_col[:], scalar=float(r), in1=w_col[:],
                                            op0=ALU.is_equal, op1=ALU.mult))
            link(v.tensor_copy(dst_int[:], k.dst_col[:]))
            link(v.tensor_scalar(digit_i[0][:], dst_int[:], 12, None, ALU.arith_shift_right))
            link(v.tensor_scalar(digit_i[1][:], dst_int[:], 7, DIGIT - 1, ALU.arith_shift_right, ALU.bitwise_and))
            for i in range(2):
                link(v.tensor_copy(digit_f[i][:], digit_i[i][:]))
            for i in range(2):
                for d in range(DIGIT):
                    ins = v.tensor_scalar(hot[i][:, :, d], digit_f[i][:], float(d), None, ALU.is_equal)
                    if d < DIGIT - 1:
                        made[0] += 1
                        ins.then_inc(dve_step, 1)
                link(ins, hot_ready)
            dve.wait_ge(counted, 1)
            link(v.tensor_copy(counts[:], small[0:DIGIT, 3, 0:DIGIT]))
            link(v.tensor_tensor_scan(running[:], zeros_d[:], counts[:], 0.0, ALU.add, ALU.add), running_ready)
            dve.wait_ge(offsets_done, 1)
            link(v.tensor_tensor(starts[:], running[:], counts[:], ALU.subtract))
            link(v.tensor_scalar(starts[:], starts[:], small[0:DIGIT, 3, 64:65], None, ALU.add), starts_ready)
            dve.wait_ge(descents_summed, 1)
            link(v.tensor_scalar(flag[:, 0:1], small[0:1, 0, 200:201], 0.5, None, ALU.is_gt))
            link(v.tensor_scalar(flag[:, 1:2], flag[:, 0:1], -1.0, 1.0, ALU.mult, ALU.add))
            dve.wait_ge(row_loaded, 32)
            B = s.batches
            per = TPB // PAIRS
            every = lambda first, n: row[:, first:first + s.tiles].rearrange("o (b j) -> o b j", j=n)
            pair_start = every(0, per)[:, :, 0].rearrange("o (b i) -> o b i", i=PAIRS)
            pair_end = every(per, per)[:, :, 0].rearrange("o (b i) -> o b i", i=PAIRS)
            batch_start = every(0, TPB)[:, :, 0]
            batch_end = every(TPB, TPB)[:, :, 0]
            link(v.tensor_tensor(size[:], pair_end, pair_start, ALU.subtract))
            link(v.tensor_reduce(crowd[:], size[:], AX.X, ALU.max))
            link(v.tensor_scalar(wide[:], crowd[:], float(P), flag[:, 0:1], ALU.is_gt, ALU.max))
            link(v.tensor_scalar(crowd[:], crowd[:], float(WIDE), flag[:, 0:1], ALU.is_gt, ALU.max))
            link(v.tensor_scalar(calm[:], crowd[:], -1.0, 1.0, ALU.mult, ALU.add))
            link(v.tensor_tensor(scratch[:], batch_end, batch_start, ALU.subtract))
            link(v.tensor_scalar(scratch[:], scratch[:], float(BLOCK - 1), None, ALU.add))
            link(v.tensor_copy(scratch_i[:], scratch[:]))
            link(v.tensor_scalar(scratch_i[:], scratch_i[:], 9, None, ALU.arith_shift_right))
            link(v.tensor_copy(scratch[:], scratch_i[:]))
            link(v.tensor_tensor(scratch[:], scratch[:], crowd[:], ALU.mult))
            link(v.tensor_scalar(scratch[:], scratch[:], flag[:, 1:2], None, ALU.mult))
            link(v.tensor_scalar(need_f[:], crowd[:], flag[:, 0:1], float(NB), ALU.mult, ALU.mult))
            link(v.tensor_tensor(scratch[:], scratch[:], need_f[:], ALU.add))
            link(v.tensor_tensor(scratch[:], scratch[:], wide[:], ALU.add))
            link(v.tensor_copy(k.kind[:], scratch[:]))
            table = k.table[:].rearrange("o (b j) -> o b j", j=4)
            link(v.tensor_scalar(scratch[:], batch_start, flag[:, 1:2], float(s.first_row), ALU.mult, ALU.add))
            link(v.tensor_copy(table[:, :, 0], scratch[:]))
            link(v.tensor_copy(need_i[:], batch_end))
            link(v.tensor_scalar(need_i[:], need_i[:], 9, None, ALU.arith_shift_right))
            link(v.tensor_copy(scratch[:], need_i[:]))
            link(v.tensor_scalar(need_f[:], crowd[:], flag[:, 0:1], float(NB), ALU.mult, ALU.mult))
            link(v.tensor_scalar(scratch[:], scratch[:], 2.0, float(NB), ALU.add, ALU.min))
            link(v.tensor_tensor(scratch[:], scratch[:], need_f[:], ALU.max))
            link(v.tensor_copy(table[:, :, 1], scratch[:]))
            for i in range(PAIRS):
                link(v.tensor_scalar(scratch[:], pair_start[:, :, i], float(s.first_row), None, ALU.add))
                link(v.tensor_tensor(scratch[:], scratch[:], calm[:], ALU.mult))
                link(v.tensor_copy(table[:, :, 2 + i], scratch[:]))
            for r in range(2):
                link(v.tensor_copy(part[r][0][:], bias_f[r][:]))
                link(v.tensor_tensor(left[r][0][:], bias_f[r][:], part[r][0][:], ALU.subtract))
                link(v.tensor_copy(part[r][1][:], left[r][0][:]))
                link(v.tensor_tensor(left[r][1][:], left[r][0][:], part[r][1][:], ALU.subtract))
                link(v.tensor_copy(part[r][2][:], left[r][1][:]))
                link(v.tensor_scalar(pick[r][0][:], part[r][0][:], k.ident[0:3, 0:1], None, ALU.mult))
                for j in (1, 2):
                    link(v.scalar_tensor_tensor(out=pick[r][j % 2][:], in0=part[r][j][:],
                                                scalar=k.ident[0:3, j:j + 1], in1=pick[r][(j + 1) % 2][:],
                                                op0=ALU.mult, op1=ALU.add))
                for j in range(TPB):
                    link(v.tensor_copy(k.bias[r][:, P * j:P * (j + 1)], pick[r][0][:]))

        @block.tensor
        def _(pe):
            pe.wait_ge(consts, 5)
            pe.wait_ge(floats_ready, 1)
            for n in range(4):
                edges = raw_f[n][:].rearrange("b (p c) -> b c p", c=CPB)
                for c in range(CPB):
                    last = nc.tensor.transpose(tp[:, n, P * c:P * c + NB], edges[:, c, :], k.ident[0:NB, 0:NB])
            last.then_inc(turned, 1)
            pe.wait_ge(extremes_ready, 1)
            nc.tensor.transpose(small[0:2, 0, 0:P], extremes[:], k.ident[:])
            nc.tensor.transpose(small[:, 1, 0:P], raw_m[:], k.ident[:]).then_inc(extremes_turned, 1)
            pe.wait_ge(diagonal_ready, 1)
            nc.tensor.matmul(small[:, 2, 0:2], ones[0:2, :], ext_d[:], start=True, stop=True).then_inc(extremes_spread, 1)
            pe.wait_ge(hot_ready, 2)
            for q in range(NB * CPB):
                last = nc.tensor.matmul(small[0:DIGIT, 3, 0:DIGIT], hot[0][:, q, :], hot[1][:, q, :],
                                        start=(q == 0), stop=(q == NB * CPB - 1))
            last.then_inc(counted, 1)
            pe.wait_ge(running_ready, 1)
            nc.tensor.matmul(small[0:DIGIT, 3, 64:65], below[:], running[:, DIGIT - 1:DIGIT], start=True,
                             stop=True).then_inc(offsets_done, 1)
            pe.wait_ge(descents_ready, 1)
            nc.tensor.matmul(small[0:1, 0, 200:201], ones[:, 0:1], descents[:], start=True,
                             stop=True).then_inc(descents_summed, 1)


class Sums:

    def __init__(self, nc, ctx, sem, s, k, dram, name, transposed):
        self.nc, self.s, self.k, self.rows, self.transposed = nc, s, k, dram.edge_rows, transposed
        sb = lambda n, sh: ctx.enter_context(nc.sbuf_tensor(f"{name}_{n}", sh, FP32))
        self.window = sb("window", [P, UNROLL, PAIRS, WIDE // P, ROW])
        self.place = sb("place", [P, 2, PAIRS])
        self.ends = sb("ends", [P, 2, TPB, P])
        self.second_place = sb("second_place", [P, PAIRS])
        self.second_ends = sb("second_ends", [P, TPB, P])
        self.step = sb("step", [P, 2, CPH, ROW])
        self.step_place = sb("step_place", [P, 2, CPH])
        self.step_ends = sb("step_ends", [P, 2, CPH, TPB, P])
        self.loaded = [sem(f"windows_loaded{i}") for i in range(UNROLL)]
        self.placed = sem("windows_placed")
        self.built = sem("ends_built")
        self.added = sem("windows_added")
        self.second_free = sem("second_free")
        self.second_placed = sem("second_placed")
        self.second_built = sem("second_built")
        self.half_free = [sem(f"half_free{i}") for i in range(2)]
        self.half_loaded = [sem(f"half_loaded{i}") for i in range(2)]
        self.half_placed = sem("half_placed")
        self.half_built = [sem(f"half_built{i}") for i in range(2)]
        self.kinds = {}

    def kind_of(self, engine, at):
        if at.slot == 0:
            _, self.kinds[engine.engine] = self.nc.values_load_multi_w_load_instructions(
                self.k.kind[0:1, bass.ds(at.b, UNROLL)], engines=[engine.engine], min_val=0, max_val=self.s.blocks + 1,
                skip_runtime_bounds_check_because="worked out on the chip from counts of the edges")
        return self.kinds[engine.engine][at.slot]

    def load(self, sp, at, stored):
        _, (first, need, *starts) = self.nc.values_load_multi_w_load_instructions(
            self.k.table[0:1, bass.ds(at.b * 4, 4)], engines=[sp.engine], min_val=0, max_val=self.s.rows - BLOCK,
            skip_runtime_bounds_check_because="counts of edges behind the first padding, which a block of padding follows")
        kind = self.kind_of(sp, at)
        if stored is not None:
            sp.wait_ge(stored, self.nc.s_assert_within(need, 1, self.s.blocks))
            sp.sem_inc(self.k.passed, 1)
        if at.at_least(UNROLL):
            sp.wait_ge(self.added, at.b - UNROLL + 1)
        sp.sem_inc(self.k.passed, 1)
        with sp.If(kind > 0):
            for i in range(PAIRS):
                sp.dma_start(self.window[:, at.slot, i],
                             self.rows[bass.ds(starts[i], WIDE), :].rearrange("(c p) r -> p c r", p=P)
                             ).then_inc(self.loaded[at.slot], 16)
        with sp.Else():
            for i in range(PAIRS):
                sp.dma_start(self.window[:, at.slot, i, 0], self.rows[bass.ds(starts[i], P), :]
                             ).then_inc(self.loaded[at.slot], 16)
        with sp.If(kind > 1):
            with sp.Fori(1, kind) as x:
                for h in range(2):
                    row = self.nc.s_assert_within(
                        first + (x - 1) * BLOCK + h * (BLOCK // 2), 0, self.s.rows - BLOCK // 2,
                        skip_runtime_bounds_check_because="a block of padding follows the batch's rows")
                    sp.wait_ge(self.half_free[h], 1)
                    sp.sem_clear(self.half_free[h])
                    sp.dma_start(self.step[:, h], self.rows[bass.ds(row, BLOCK // 2), :]
                                 .rearrange("(p c) r -> p c r", c=CPH)).then_inc(self.half_loaded[h], 16)

    def begin(self, dve):
        dve.sem_inc(self.second_free, 1)
        for h in range(2):
            dve.sem_inc(self.half_free[h], 1)

    def match(self, ends, place, pair):
        split = lambda t: t.rearrange("p (i n) -> p i n", i=PAIRS)[:, pair]
        return self.nc.vector.tensor_scalar(split(ends.rearrange("p t n -> p (t n)")), split(self.k.node[:]), place,
                                            None, ALU.is_equal)

    def build(self, dve, at):
        nc, k, h2 = self.nc, self.k, at.slot % 2
        base = k.base[:, bass.ds(at.b, 1)]
        kind = self.kind_of(dve, at)
        with dve.If(kind > 1):
            with dve.Fori(1, kind) as x:
                for h in range(2):
                    dve.wait_ge(self.half_loaded[h], 16)
                    dve.sem_clear(self.half_loaded[h])
                    nc.vector.tensor_scalar(self.step_place[:, h], self.step[:, h, :, P], base, None,
                                            ALU.subtract).then_inc(self.half_placed, 1)
                    dve.wait_ge(self.half_placed, 1)
                    dve.sem_clear(self.half_placed)
                    for c in range(CPH):
                        last = nc.vector.tensor_scalar(self.step_ends[:, h, c].rearrange("p t n -> p (t n)"), k.node[:],
                                                       self.step_place[:, h, c:c + 1], None, ALU.is_equal)
                    last.then_inc(self.half_built[h], 1)
        dve.wait_ge(self.loaded[at.slot], (at.turn + 1) * 16 * PAIRS)
        nc.vector.tensor_scalar(self.place[:, h2], self.window[:, at.slot, :, 0, P], base, None,
                                ALU.subtract).then_inc(self.placed, 1)
        dve.wait_ge(self.placed, at.b + 1)
        if at.at_least(2):
            dve.wait_ge(self.added, at.b - 1)
        for i in range(PAIRS):
            last = self.match(self.ends[:, h2], self.place[:, h2, i:i + 1], i)
        last.then_inc(self.built, 1)
        with dve.If(kind > 0):
            dve.wait_ge(self.second_free, 1)
            dve.sem_clear(self.second_free)
            nc.vector.tensor_scalar(self.second_place[:], self.window[:, at.slot, :, 1, P], base, None,
                                    ALU.subtract).then_inc(self.second_placed, 1)
            dve.wait_ge(self.second_placed, 1)
            dve.sem_clear(self.second_placed)
            for i in range(PAIRS):
                last = self.match(self.second_ends[:], self.second_place[:, i:i + 1], i)
            last.then_inc(self.second_built, 1)

    def products(self, bank, ends, rows, tiles):
        if self.transposed:
            return self.nc.tensor.matmul(bank[:, tiles.start:tiles.stop].rearrange("p t n -> p (t n)"), rows,
                                         ends[:, tiles.start:tiles.stop].rearrange("p t n -> p (t n)"), start=False,
                                         stop=True, skip_group_check=True)
        for j in tiles:
            last = self.nc.tensor.matmul(bank[:, j], ends[:, j], rows, start=False, stop=True, skip_group_check=True)
        return last

    def add(self, pe, at, bank):
        kind = self.kind_of(pe, at)
        tiles = [range(i * TPB // PAIRS, (i + 1) * TPB // PAIRS) for i in range(PAIRS)]
        with pe.If(kind > 0):
            with pe.If(kind > 1):
                with pe.Fori(1, kind) as x:
                    for h in range(2):
                        pe.wait_ge(self.half_built[h], 1)
                        pe.sem_clear(self.half_built[h])
                        for c in range(CPH):
                            last = self.products(bank, self.step_ends[:, h, c], self.step[:, h, c, 0:P], range(TPB))
                        last.then_inc(self.half_free[h], 1)
            pe.wait_ge(self.second_built, 1)
            pe.sem_clear(self.second_built)
            for i in range(PAIRS):
                last = self.products(bank, self.second_ends, self.window[:, at.slot, i, 1, 0:P], tiles[i])
            last.then_inc(self.second_free, 1)
        pe.wait_ge(self.built, at.b + 1)
        for i in range(PAIRS):
            last = self.products(bank, self.ends[:, at.slot % 2], self.window[:, at.slot, i, 0, 0:P], tiles[i])
        last.then_inc(self.added, 1)


def stage_index(nc, k, at, index, staged):
    nc.gpsimd.tensor_copy(index[:, at.slot, :], k.src_col[:, bass.ds(at.b * CPB, CPB)]).then_inc(staged, 1)


def gather_block(nc, pool, k, table, ring, at, index, staged, gathered):
    pool.wait_ge(staged, at.b + 1)
    pool.sem_inc(k.passed, 1)
    for c in range(CPB):
        nc.gpsimd.indirect_dma_start(
            out=ring[:, at.slot, c, 0:P], out_offset=None, in_=table,
            in_offset=bass.IndirectOffsetOnAxis(ap=index[:, at.slot, c:c + 1], axis=0)).then_inc(gathered[at.slot], 16)


def block_rows(dram, s, at):
    return dram.edge_rows[bass.ds(at.b * BLOCK + s.first_row, BLOCK), :].rearrange("(p c) r -> p (c r)", c=CPB)


class Norm:

    def __init__(self, nc, ctx, sem, name):
        self.nc = nc
        sb = lambda n, sh: ctx.enter_context(nc.sbuf_tensor(f"{name}_{n}", sh, FP32))
        self.v = sb("to_norm", [P, 2, TPB, P])
        self.stats = sb("bn_stats", [P, 2, TPB, nc.vector.BN_STATS_DIM])
        self.moments = sb("moments", [P, 2, TPB, nc.vector.BN_AGGR_DIM])
        self.std = sb("std", [P, 2, TPB])
        self.rstd = sb("rstd", [P, 2, TPB])
        self.shift = sb("shift", [P, 2, TPB])
        self.eps = sb("eps", [P, 1])
        self.out = sb("normed", [P, UNROLL, TPB, P])
        self.summed = sem("summed")
        self.stats_done = sem("stats_done")
        self.moments_begun = sem("moments_begun")
        self.moments_done = sem("moments_done")
        self.std_done = sem("std_done")
        self.rstd_done = sem("rstd_done")
        self.shift_done = sem("shift_done")
        self.normed = sem("normed")
        self.eps_made = sem("eps_made")

    def constants(self):
        self.nc.vector.memset(self.eps[:], LN_EPS).then_inc(self.eps_made, 1)

    def statistics(self, dve, at, update, rows):
        nc, h = self.nc, at.slot % 2
        if at.at_least(2):
            dve.wait_ge(self.normed, (at.b - 1) * TPB)
        nc.vector.tensor_tensor(self.v[:, h], update, rows, ALU.add).then_inc(self.summed, 1)
        dve.wait_ge(self.summed, at.b + 1)
        for j in range(TPB):
            nc.vector.bn_stats(self.stats[:, h, j, :], self.v[:, h, j, :]).then_inc(self.stats_done, 1)
        dve.wait_ge(self.stats_done, (at.b + 1) * TPB)
        dve.sem_inc(self.moments_begun, 1)
        for j in range(TPB):
            nc.vector.bn_aggr(self.moments[:, h, j, :], self.stats[:, h, j, :]).then_inc(self.moments_done, 1)

    def deviation(self, act, at):
        h = at.slot % 2
        act.wait_ge(self.moments_done, (at.b + 1) * TPB)
        if at.at_least(2):
            act.wait_ge(self.rstd_done, at.b - 1)
        self.nc.scalar.activation(self.std[:, h, :], self.moments[:, h, :, 1], ACT.Sqrt,
                                  bias=self.eps[:]).then_inc(self.std_done, 1)

    def factors(self, dve, at):
        nc, h = self.nc, at.slot % 2
        dve.wait_ge(self.std_done, at.b + 1)
        nc.vector.reciprocal(self.rstd[:, h, :], self.std[:, h, :]).then_inc(self.rstd_done, 1)
        dve.wait_ge(self.rstd_done, at.b + 1)
        nc.vector.scalar_tensor_tensor(out=self.shift[:, h, :], in0=self.moments[:, h, :, 0], scalar=-1.0,
                                       in1=self.rstd[:, h, :], op0=ALU.mult, op1=ALU.mult).then_inc(self.shift_done, 1)

    def apply(self, act, at, stored):
        h = at.slot % 2
        act.wait_ge(self.shift_done, at.b + 1)
        if at.at_least(UNROLL):
            act.wait_ge(stored[at.slot], at.turn * 16)
        for j in range(TPB):
            self.nc.scalar.activation(self.out[:, at.slot, j, :], self.v[:, h, j, :], ACT.Identity,
                                      bias=self.shift[:, h, j:j + 1],
                                      scale=self.rstd[:, h, j:j + 1]).then_inc(self.normed, 1)


def batch_rows(array, at):
    start = at.b * (TPB * P)
    return array[bass.ds(start, TPB * P), :].rearrange("(t p) f -> p t f", p=P)


def load_batch(sp, s, k, array, at, ring, loaded, zeroed):
    out = ring[:, at.slot]
    if not isinstance(at.b, int) or at.b < s.batches - 1 or s.tail == TPB * P:
        sp.dma_start(out, batch_rows(array, at)).then_inc(loaded[at.slot], 16)
        return
    whole, rest = divmod(s.tail, P)
    base = at.b * TPB * P
    sp.dma_start(out[:, whole:TPB], k.zeros[:, 0:(TPB - whole) * P].rearrange("p (t f) -> p t f", f=P)).then_inc(zeroed, 16)
    sp.wait_ge(zeroed, 16)
    parts = []
    if whole:
        parts.append((out[:, 0:whole], array[base:base + whole * P, :].rearrange("(t p) f -> p t f", p=P)))
    if rest:
        parts.append((out[0:rest, whole], array[base + whole * P:s.nodes, :]))
    for n, (o, i) in enumerate(parts):
        if n < len(parts) - 1:
            sp.dma_start(o, i).then_inc(zeroed, 16)
            sp.wait_ge(zeroed, 32 + 16 * n)
        else:
            sp.dma_start(o, i).then_inc(loaded[at.slot], 16)


def store_batch(sp, s, array, at, ring, stored, padded):
    src = ring[:, at.slot]
    if padded or not isinstance(at.b, int) or at.b < s.batches - 1 or s.tail == TPB * P:
        sp.dma_start(batch_rows(array, at), src).then_inc(stored[at.slot], 16)
        return
    whole, rest = divmod(s.tail, P)
    base = at.b * TPB * P
    if whole:
        sp.dma_start(array[base:base + whole * P, :].rearrange("(t p) f -> p t f", p=P),
                     src[:, 0:whole]).then_inc(stored[at.slot], 16)
    if rest:
        sp.dma_start(array[base + whole * P:s.nodes, :], src[0:rest, whole]).then_inc(stored[at.slot], 16)


def wait_stored(sp, s, stored, padded):
    pieces = 1 if padded or s.tail == TPB * P else (s.tail >= P) + (s.tail % P > 0)
    for slot in range(UNROLL):
        n = len(range(slot, s.batches, UNROLL))
        last = slot == (s.batches - 1) % UNROLL
        sp.wait_ge(stored[slot], 16 * (n + (pieces - 1 if last else 0)))


def first_phase(nc, s, k, dram):
    with ExitStack() as ctx:
        sem = ctx.enter_context(phase_semaphores(nc, "l0_"))
        sums = Sums(nc, ctx, sem, s, k, dram, "l0", True)
        norm = Norm(nc, ctx, sem, "l0")
        sb = lambda n, sh, dt=FP32: ctx.enter_context(nc.sbuf_tensor(n, sh, dt))
        ps = lambda n: ctx.enter_context(nc.psum_tensor(n, [P, TPB, P], FP32))
        x_ring = sb("x_ring", [P, UNROLL, TPB, P])
        zt = sb("zt", [P, 2, TPB, P])
        index = sb("l0_index", [P, RING, CPB], I32)
        gather_ring = sb("gather_ring", [P, RING, CPB, ROW])
        zt_ps = [ps(f"zt_ps{i}") for i in range(2)]
        update_ps = [ps(f"update{i}") for i in range(2)]
        x_loaded = [sem(f"x_loaded{i}") for i in range(UNROLL)]
        x_zeroed = sem("x_zeroed")
        stored = [sem(f"x1_stored{i}") for i in range(UNROLL)]
        gathered = [sem(f"x_gathered{i}") for i in range(RING)]
        staged = sem("l0_index_staged")
        rows_stored = [sem(f"l0_rows_stored{i}") for i in range(RING)]
        blocks_stored = sem("l0_blocks_stored")
        marked = sem("l0_marked")
        zt_done = sem("zt_copied")
        update_done = sem("update_done")
        B = s.batches
        block = ctx.enter_context(nc.Block())

        @block.sync
        def _(sp):
            def body(at):
                if at.within(B):
                    if at.at_least(UNROLL):
                        sp.wait_ge(norm.summed, at.b - UNROLL + 1)
                        sp.sem_inc(k.passed, 1)
                    load_batch(sp, s, k, dram.x, at, x_ring, x_loaded, x_zeroed)
                    sums.load(sp, at, blocks_stored)
                out = at.back(UNROLL)
                if out.within(B):
                    sp.wait_ge(norm.normed, (out.b + 1) * TPB)
                    sp.sem_inc(k.passed, 1)
                    store_batch(sp, s, dram.x1, out, norm.out, stored, True)

            each(sp, body, B, drain=UNROLL)
            wait_stored(sp, s, stored, True)

        @block.gpsimd
        def _(pool):
            nc.gpsimd.memset(gather_ring[:], 0.0).then_inc(marked, 1)
            pool.wait_ge(marked, 1)

            def body(at):
                store = at.back(1)
                if store.within(s.blocks):
                    pool.wait_ge(marked, store.b + 2)
                    pool.sem_inc(k.passed, 1)
                    pool.wait_ge(gathered[store.slot], (store.turn + 1) * 16 * CPB)
                    pool.dma_start(block_rows(dram, s, store), gather_ring[:, store.slot].rearrange("p c r -> p (c r)")
                                   ).then_inc(rows_stored[store.slot], 16)
                told = at.back(3)
                if told.within(s.blocks):
                    pool.wait_ge(rows_stored[told.slot], (told.turn + 1) * 16)
                    pool.sem_inc(blocks_stored, 1)
                after = at.ahead(1)
                if after.within(s.blocks):
                    if after.at_least(RING):
                        pool.wait_ge(gathered[after.slot], after.turn * 16 * CPB)
                    stage_index(nc, k, after, index, staged)
                if at.within(s.blocks):
                    if at.at_least(RING):
                        pool.wait_ge(rows_stored[at.slot], at.turn * 16)
                    nc.gpsimd.tensor_copy(gather_ring[:, at.slot, :, P],
                                          k.dst_col[:, bass.ds(at.b * CPB, CPB)]).then_inc(marked, 1)
                    gather_block(nc, pool, k, dram.x, gather_ring, at, index, staged, gathered)

            stage_index(nc, k, At(0, 0, 0), index, staged)
            each(pool, body, s.blocks, drain=3)

        @block.vector
        def _(dve):
            norm.constants()
            sums.begin(dve)

            def body(at):
                if at.within(B):
                    sums.build(dve, at)
                if at.back(3).within(B):
                    norm.factors(dve, at.back(3))
                two = at.back(2)
                if two.within(B):
                    dve.wait_ge(update_done, two.b + 1)
                    norm.statistics(dve, two, update_ps[two.slot % 2][:], x_ring[:, two.slot])

            each(dve, body, B, drain=3)

        @block.tensor
        def _(pe):
            def body(at):
                if at.within(B):
                    bank = zt_ps[at.slot % 2]
                    pe.wait_ge(x_loaded[at.slot], (at.turn + 1) * 16)
                    if at.at_least(2):
                        pe.wait_ge(zt_done, at.b - 1)
                    for j in range(TPB):
                        nc.tensor.matmul(bank[:, j], x_ring[:, at.slot, j], k.ident[:], start=(j == 0), stop=True,
                                         skip_group_check=True)
                    sums.add(pe, at, bank)
                prev = at.back(1)
                if prev.within(B):
                    pe.wait_ge(zt_done, prev.b + 1)
                    if prev.at_least(2):
                        pe.wait_ge(norm.summed, prev.b - 1)
                    for j in range(TPB):
                        last = nc.tensor.matmul(update_ps[prev.slot % 2][:, j], zt[:, prev.slot % 2, j], k.w0t[:],
                                                start=True, stop=True)
                    last.then_inc(update_done, 1)

            each(pe, body, B, drain=1)

        @block.scalar
        def _(act):
            act.wait_ge(norm.eps_made, 1)

            def body(at):
                prev = at.back(1)
                if at.back(3).within(B):
                    norm.apply(act, at.back(3), stored)
                if prev.within(B):
                    act.wait_ge(sums.added, prev.b + 1)
                    if prev.at_least(2):
                        act.wait_ge(update_done, prev.b - 1)
                    nc.scalar.copy(zt[:, prev.slot % 2], zt_ps[prev.slot % 2][:]).then_inc(zt_done, 1)
                if at.back(2).within(B):
                    norm.deviation(act, at.back(2))

            each(act, body, B, drain=3)


def message_phase(nc, s, k, dram, layer, table):
    name = f"m{layer}"
    with ExitStack() as ctx:
        sem = ctx.enter_context(phase_semaphores(nc, f"{name}_"))
        sb = lambda n, sh, dt=FP32: ctx.enter_context(nc.sbuf_tensor(f"{name}_{n}", sh, dt))
        ring = sb("rows_ring", [P, RING, CPB, P])
        index = sb("index", [P, RING, CPB], I32)
        rows_t = sb("rows_t", [P, 2, P])
        partial = sb("partial", [P, 2, 3, P])
        messages = sb("messages", [P, RING, CPB, ROW])
        turned_ps = ctx.enter_context(nc.psum_tensor(f"{name}_turned_ps", [P, 2, 4 * P], FP32))
        product_ps = ctx.enter_context(nc.psum_tensor(f"{name}_product_ps", [P, CPB, 4 * P], FP32))
        gathered = [sem(f"gathered{i}") for i in range(RING)]
        stored = [sem(f"stored{i}") for i in range(RING)]
        staged = sem("index_staged")
        turned = sem("turned")
        rows_t_done = sem("rows_t_copied")
        product_done = sem("product_done")
        part0_done = sem("part0_done")
        added = sem("parts_added")
        message_done = sem("message_done")
        cleared = sem("cleared")
        marked = sem("marked")
        wrel = k.wrel[layer]
        B = s.blocks
        coef = lambda c, r: k.coef[:, bass.ds(c * RELATIONS + r, 1)]
        block = ctx.enter_context(nc.Block())

        @block.gpsimd
        def _(pool):
            def body(at):
                after = at.ahead(1)
                if after.within(B):
                    if after.at_least(RING):
                        pool.wait_ge(gathered[after.slot], after.turn * 16 * CPB)
                    stage_index(nc, k, after, index, staged)
                if at.at_least(RING):
                    pool.wait_ge(turned, (at.b - RING + 1) * CPB)
                    pool.sem_inc(k.passed, 1)
                gather_block(nc, pool, k, table, ring, at, index, staged, gathered)

            stage_index(nc, k, At(0, 0, 0), index, staged)
            each(pool, body, B)

        @block.tensor
        def _(pe):
            def turn(at, i):
                c = at.b * CPB + i
                if i == 0:
                    pe.wait_ge(gathered[at.slot], (at.turn + 1) * 16 * CPB)
                if at.at_least(1) or i >= 2:
                    pe.wait_ge(rows_t_done, c - 1)
                nc.tensor.transpose(turned_ps[:, i % 2, 0:P], ring[:, at.slot, i],
                                    k.ident[:]).then_inc(turned, 1)

            def body(at):
                for i in range(CPB):
                    c = at.b * CPB + i
                    if i < CPB - 1:
                        turn(at, i + 1)
                    elif at.ahead(1).within(B):
                        turn(at.ahead(1), 0)
                    pe.wait_ge(rows_t_done, c + 1)
                    if at.at_least(1):
                        pe.wait_ge(message_done, c - CPB + 1)
                    nc.tensor.matmul(product_ps[:, i], rows_t[:, i % 2], wrel[:], start=True,
                                     stop=True).then_inc(product_done, 1)

            turn(At(0, 0, 0), 0)
            each(pe, body, B)

        @block.scalar
        def _(act):
            def copy_rows(c, i):
                act.wait_ge(turned, c + 1)
                if not isinstance(c, int) or c >= 2:
                    act.wait_ge(product_done, c - 1)
                nc.scalar.copy(rows_t[:, i % 2], turned_ps[:, i % 2, 0:P]).then_inc(rows_t_done, 1)

            def body(at):
                for i in range(CPB):
                    c = at.b * CPB + i
                    last = isinstance(at.b, int) and at.b == B - 1 and i == CPB - 1
                    if not last:
                        copy_rows(c + 1, i + 1)
                    act.wait_ge(product_done, c + 1)
                    if at.at_least(1) or i >= 2:
                        act.wait_ge(message_done, c - 1)
                    nc.scalar.activation(partial[:, i % 2, 0], product_ps[:, i, 0:P], ACT.Copy,
                                         scale=coef(c, 0)).then_inc(part0_done, 1)

            copy_rows(0, 0)
            each(act, body, B)

        @block.vector
        def _(dve):
            nc.vector.memset(messages[:], 0.0).then_inc(cleared, 1)
            dve.wait_ge(cleared, 1)

            def body(at):
                for i in range(CPB):
                    c = at.b * CPB + i
                    dve.wait_ge(part0_done, c + 1)
                    for r in (1, 2):
                        nc.vector.scalar_tensor_tensor(
                            out=partial[:, i % 2, r], in0=product_ps[:, i, r * P:(r + 1) * P], scalar=coef(c, r),
                            in1=partial[:, i % 2, r - 1], op0=ALU.mult, op1=ALU.add).then_inc(added, 1)
                        dve.wait_ge(added, 2 * c + r)
                    if i == 0:
                        if at.at_least(RING):
                            dve.wait_ge(stored[at.slot], at.turn * 16)
                        nc.vector.tensor_copy(messages[:, at.slot, :, P],
                                              k.dst_col[:, bass.ds(at.b * CPB, CPB)]).then_inc(marked, 1)
                    nc.vector.scalar_tensor_tensor(
                        out=messages[:, at.slot, i, 0:P], in0=product_ps[:, i, 3 * P:4 * P], scalar=coef(c, 3),
                        in1=partial[:, i % 2, 2], op0=ALU.mult, op1=ALU.add).then_inc(message_done, 1)

            each(dve, body, B)

        @block.sync
        def _(sp):
            def body(at):
                sp.wait_ge(marked, at.b + 1)
                sp.sem_inc(k.passed, 1)
                sp.wait_ge(message_done, (at.b + 1) * CPB)
                sp.sem_inc(k.passed, 1)
                sp.dma_start(block_rows(dram, s, at),
                             messages[:, at.slot].rearrange("p c r -> p (c r)")).then_inc(stored[at.slot], 16)

            each(sp, body, B)
            for slot in range(RING):
                sp.wait_ge(stored[slot], 16 * len(range(slot, B, RING)))


def conv_phase(nc, s, k, dram, layer, table, out):
    name = f"c{layer}"
    normed = layer == 1
    with ExitStack() as ctx:
        sem = ctx.enter_context(phase_semaphores(nc, f"{name}_"))
        sums = Sums(nc, ctx, sem, s, k, dram, name, False)
        norm = Norm(nc, ctx, sem, name) if normed else None
        sb = lambda n, sh, dt=FP32: ctx.enter_context(nc.sbuf_tensor(f"{name}_{n}", sh, dt))
        ps = lambda n: ctx.enter_context(nc.psum_tensor(f"{name}_{n}", [P, TPB, P], FP32))
        rows = sb("rows", [P, UNROLL, TPB, P])
        residual = sb("residual", [P, UNROLL, TPB, P]) if normed else None
        rows_t = sb("rows_t", [P, 2, TPB, P])
        relu = None if normed else sb("relu", [P, UNROLL, TPB, P])
        rows_t_ps = [ps(f"rows_t_ps{i}") for i in range(2)]
        sums_ps = [ps(f"sums{i}") for i in range(2)]
        rows_loaded = [sem(f"rows_loaded{i}") for i in range(UNROLL)]
        residual_loaded = [sem(f"residual_loaded{i}") for i in range(UNROLL)]
        stored = [sem(f"stored{i}") for i in range(UNROLL)]
        turned = sem("rows_turned")
        rows_t_done = sem("rows_t_copied")
        own_done = sem("own_product_done")
        relu_done = sem("relu_done")
        B = s.batches
        block = ctx.enter_context(nc.Block())
        finished = (lambda b: (norm.summed, b + 1)) if normed else (lambda b: (relu_done, b + 1))

        @block.sync
        def _(sp):
            def body(at):
                if at.within(B):
                    if at.at_least(UNROLL):
                        sp.wait_ge(turned, at.b - UNROLL + 1)
                        sp.sem_inc(k.passed, 1)
                    sp.dma_start(rows[:, at.slot], batch_rows(table, at)).then_inc(rows_loaded[at.slot], 16)
                    if normed:
                        if at.at_least(UNROLL):
                            sp.wait_ge(norm.summed, at.b - UNROLL + 1)
                            sp.sem_inc(k.passed, 1)
                        sp.dma_start(residual[:, at.slot],
                                     batch_rows(dram.x1, at)).then_inc(residual_loaded[at.slot], 16)
                    sums.load(sp, at, None)
                done = at.back(UNROLL if normed else 3)
                if done.within(B):
                    if normed:
                        sp.wait_ge(norm.normed, (done.b + 1) * TPB)
                    else:
                        sp.wait_ge(relu_done, done.b + 1)
                    sp.sem_inc(k.passed, 1)
                    store_batch(sp, s, out, done, norm.out if normed else relu, stored, not normed)

            each(sp, body, B, drain=UNROLL)
            wait_stored(sp, s, stored, not normed)

        @block.vector
        def _(dve):
            if normed:
                norm.constants()
            sums.begin(dve)

            def body(at):
                if at.within(B):
                    sums.build(dve, at)
                if not normed:
                    return
                if at.back(2).within(B):
                    norm.factors(dve, at.back(2))
                prev = at.back(1)
                if prev.within(B):
                    dve.wait_ge(own_done, prev.b + 1)
                    dve.wait_ge(residual_loaded[prev.slot], (prev.turn + 1) * 16)
                    norm.statistics(dve, prev, sums_ps[prev.slot % 2][:], residual[:, prev.slot])

            each(dve, body, B, drain=2)

        @block.tensor
        def _(pe):
            def turn(at):
                pe.wait_ge(rows_loaded[at.slot], (at.turn + 1) * 16)
                if at.at_least(2):
                    pe.wait_ge(rows_t_done, at.b - 1)
                for j in range(TPB):
                    last = nc.tensor.transpose(rows_t_ps[at.slot % 2][:, j], rows[:, at.slot, j], k.ident[:])
                last.then_inc(turned, 1)

            def body(at):
                bank = sums_ps[at.slot % 2]
                if at.at_least(2):
                    sem_, n = finished(at.b - 2)
                    pe.wait_ge(sem_, n)
                nc.tensor.matmul(bank[:].rearrange("p t f -> p (t f)"), k.ones3[:], k.bias[layer][:], start=True,
                                 stop=True, skip_group_check=True)
                sums.add(pe, at, bank)
                if at.ahead(1).within(B):
                    turn(at.ahead(1))
                pe.wait_ge(rows_t_done, at.b + 1)
                for j in range(TPB):
                    last = nc.tensor.matmul(bank[:, j], rows_t[:, at.slot % 2, j], k.root[layer][:], start=False,
                                            stop=True, skip_group_check=True)
                last.then_inc(own_done, 1)

            turn(At(0, 0, 0))
            each(pe, body, B)

        @block.scalar
        def _(act):
            if normed:
                act.wait_ge(norm.eps_made, 1)

            def body(at):
                if normed and at.back(3).within(B):
                    norm.apply(act, at.back(3), stored)
                if at.within(B):
                    act.wait_ge(turned, at.b + 1)
                    if at.at_least(2):
                        act.wait_ge(own_done, at.b - 1)
                    nc.scalar.copy(rows_t[:, at.slot % 2], rows_t_ps[at.slot % 2][:]).then_inc(rows_t_done, 1)
                if normed and at.back(2).within(B):
                    norm.deviation(act, at.back(2))
                prev = at.back(1)
                if not normed and prev.within(B):
                    act.wait_ge(own_done, prev.b + 1)
                    if prev.at_least(UNROLL):
                        act.wait_ge(stored[prev.slot], prev.turn * 16)
                    nc.scalar.activation(relu[:, prev.slot], sums_ps[prev.slot % 2][:], ACT.Relu).then_inc(relu_done, 1)

            each(act, body, B, drain=3 if normed else 1)


class Named:
    pass


def build_program(nc, x, src, dst, edge_type, weight, w0, w1, root1, b1, w2, root2, b2, out):
    s = Shapes(x.shape[0], src.shape[0])
    dram = Named()
    dram.x, dram.src, dram.dst, dram.type, dram.w, dram.w0 = x, src, dst, edge_type, weight, w0
    dram.w1, dram.root1, dram.b1, dram.w2, dram.root2, dram.b2, dram.out = w1, root1, b1, w2, root2, b2, out
    rows = s.batches * TPB * P
    dram.x1 = nc.dram_tensor("x1_rows", (rows, P), FP32).ap()
    dram.h1 = nc.dram_tensor("h1_rows", (rows, P), FP32).ap()
    dram.edge_rows = nc.dram_tensor("edge_rows", (s.rows, ROW), FP32).ap()
    dram.starts = nc.dram_tensor("tile_starts", (1, DIGIT * DIGIT), FP32).ap()
    with ExitStack() as ctx:
        k = Named()
        sb = lambda n, sh, dt=FP32: ctx.enter_context(nc.sbuf_tensor(n, sh, dt))
        k.node = sb("node_numbers", [P, TPB * P])
        k.base = sb("batch_base", [P, s.batches])
        k.ident = sb("identity", [P, P])
        k.zeros = sb("zeros", [P, TPB * P])
        k.ones3 = sb("ones3", [3, P], BF16)
        k.dst_col = sb("dst_col", [P, s.blocks * CPB])
        k.src_col = sb("src_col", [P, s.blocks * CPB], I32)
        k.coef = sb("coef", [P, s.blocks * CPB * RELATIONS])
        k.kind = sb("batch_kind", [1, s.batches], I32)
        k.table = sb("batch_table", [1, s.batches * 4], I32)
        k.w0t = sb("w0t", [P, P])
        k.root = [sb(f"root{i}", [P, P]) for i in range(2)]
        k.wrel = [sb(f"wrel{i}", [P, RELATIONS * P]) for i in range(2)]
        k.bias = [sb(f"bias{i}", [3, TPB * P], BF16) for i in range(2)]
        k.passed = ctx.enter_context(nc.semaphore("waits_passed"))
        setup_phase(nc, s, k, dram)
        first_phase(nc, s, k, dram)
        message_phase(nc, s, k, dram, 0, dram.x1)
        conv_phase(nc, s, k, dram, 0, dram.x1, dram.h1)
        message_phase(nc, s, k, dram, 1, dram.h1)
        conv_phase(nc, s, k, dram, 1, dram.h1, dram.out)


_INS = ['x', 'src', 'dst', 'edge_type_4', 'edge_weight', 'L0_gnn_W', 'L1_gnn_W1', 'L1_gnn_root1', 'L1_gnn_b1',
        'L1_gnn_W2', 'L1_gnn_root2', 'L1_gnn_b2']


def kernel(**inputs):
    import numpy as _np
    import concourse.bacc as _bacc
    from concourse import mybir as _mybir
    from concourse.bass_utils import run_bass_kernel_spmd as _run

    nc = _bacc.Bacc("TRN2", target_bir_lowering=False, num_devices=1)
    arrays, args = {}, []
    for name in _INS:
        a = _np.ascontiguousarray(inputs[name])
        arrays[f"in_{name}"] = a
        args.append(nc.dram_tensor(f"in_{name}", a.shape, _mybir.dt.from_np(a.dtype), kind="ExternalInput").ap())
    shape = inputs['x'].shape
    args.append(nc.dram_tensor("out_rows", tuple(shape), FP32, kind="ExternalOutput").ap())
    build_program(nc, *args)
    r = _run(nc, [arrays], core_ids=[0])
    return r.results[0]["out_rows"]
```

```python
from contextlib import ExitStack, contextmanager

import concourse.bass as bass
from concourse import mybir

FP32 = mybir.dt.float32
BF16 = mybir.dt.bfloat16
I32 = mybir.dt.int32
ALU = mybir.AluOpType
ACT = mybir.ActivationFunctionType
AX = mybir.AxisListType

P = 128
TPB = 4
UNROLL = 8
PAIR = 2
KINDS = 4
PAIRS = 2
TILES_OF_PAIR = [range(0, 2), range(2, 4)]
CPB = 4
WIDE = 2 * P
BLOCK = CPB * P
RING = 4
RELATIONS = 4
ROW = P + 4
DIGIT = 32
NO_NODE = float(1 << 20)
LN_EPS = 1e-5
EW_EPS = 1e-8


class Shapes:

    def __init__(self, nodes, edges):
        self.nodes, self.edges = nodes, edges
        self.batches = -(-nodes // (P * TPB * PAIR)) * PAIR
        self.tiles = self.batches * TPB
        self.tail = nodes - (self.batches - PAIR) * TPB * P
        assert 0 < self.tail <= PAIR * TPB * P and self.tiles < DIGIT * DIGIT
        self.blocks = -(-(edges + WIDE) // BLOCK)
        assert self.blocks <= P
        self.first_row = WIDE
        self.rows = WIDE + (self.blocks + 1) * BLOCK


class At:

    def __init__(self, b, slot, turn, ring):
        self.b, self.slot, self.turn, self.ring = b, slot, turn, ring

    def ahead(self, n):
        carry, slot = divmod(self.slot + n, self.ring)
        return At(self.b + n if n >= 0 else self.b - -n, slot, self.turn + carry if carry >= 0 else self.turn - -carry,
                  self.ring)

    def back(self, n):
        return self.ahead(-n)

    def within(self, count):
        return not isinstance(self.b, int) or 0 <= self.b < count

    def at_least(self, n):
        return not isinstance(self.b, int) or self.b >= n


def each(engine, body, count, ring, drain=0):
    turns = (count - 1) // ring
    for b in range(min(ring, count)):
        body(At(b, b, 0, ring))
    if turns > 1:
        with engine.Fori(1, turns) as turn:
            for slot in range(ring):
                body(At(turn * ring + slot, slot, turn, ring))
    for b in range(ring * turns if turns > 1 else ring, count + drain):
        body(At(b, b % ring, b // ring, ring))


@contextmanager
def phase_semaphores(nc, prefix=""):
    used = []
    with ExitStack() as ctx:
        def sem(name):
            used.append(ctx.enter_context(nc.semaphore(prefix + name)))
            return used[-1]

        yield sem
        with nc.Block() as block:
            @block.gpsimd
            def _(pool):
                for each_used in used:
                    pool.sem_clear(each_used)


def setup_phase(nc, s, k, dram):
    NB = s.blocks
    full = s.edges // BLOCK
    rest = s.edges - full * BLOCK
    with ExitStack() as ctx:
        sb = lambda n, sh, dt=FP32: ctx.enter_context(nc.sbuf_tensor(n, sh, dt))
        sem = ctx.enter_context(phase_semaphores(nc))
        raw_i = [sb(f"raw_{n}", [NB, BLOCK], I32) for n in ("dst", "src", "type")]
        raw_f = [sb(f"rawf_{n}", [NB, BLOCK]) for n in ("dst", "src", "type", "weight")]
        next_i = sb("next_dst_i", [NB, BLOCK], I32)
        next_f = sb("next_dst", [NB, BLOCK])
        descents = sb("descents", [P, 1])
        raw_m = sb("raw_w0", [P, P])
        type_col = sb("type_col", [P, NB * CPB])
        w_col = sb("w_col", [P, NB * CPB])
        extremes = sb("extremes", [P, 2])
        ext_t = sb("ext_t", [2, 1])
        ext_d = sb("ext_d", [2, 2])
        ext_b = sb("ext_b", [P, 2])
        span = sb("span", [P, 2])
        ones = sb("ones_setup", [P, P])
        dst_int = sb("dst_int", [P, NB * CPB], I32)
        digit_i = [sb(f"digit_i{i}", [P, NB * CPB], I32) for i in range(2)]
        digit_f = [sb(f"digit_f{i}", [P, NB * CPB]) for i in range(2)]
        hot = [sb(f"digit_hot{i}", [P, NB * CPB, DIGIT], BF16) for i in range(2)]
        counts = sb("counts", [DIGIT, DIGIT])
        running = sb("running", [DIGIT, DIGIT])
        below = sb("below", [DIGIT, DIGIT])
        zeros_d = sb("zeros_digit", [DIGIT, DIGIT])
        starts = sb("starts", [DIGIT, DIGIT])
        row = sb("start_row", [1, DIGIT * DIGIT])
        size = sb("pair_size", [1, s.batches, PAIRS])
        crowd = sb("crowded", [1, s.batches])
        wide = sb("wide", [1, s.batches])
        calm = sb("calm", [1, s.batches])
        flag = sb("unsorted_flag", [1, 2])
        scratch = sb("table_scratch", [1, s.batches])
        scratch_i = sb("table_scratch_i", [1, s.batches], I32)
        need_i = sb("need_i", [1, s.batches], I32)
        need_f = sb("need_f", [1, s.batches])
        pads = sb("pad_rows", [P, CPB * ROW])
        bias_f = [sb(f"bias_f{i}", [3, P]) for i in range(2)]
        part = [[sb(f"part{i}{j}", [3, P], BF16) for j in range(3)] for i in range(2)]
        left = [[sb(f"left{i}{j}", [3, P]) for j in range(2)] for i in range(2)]
        pick = [[sb(f"pick{i}{j}", [3, P]) for j in range(2)] for i in range(2)]
        tp = ctx.enter_context(nc.psum_tensor("tp_setup", [P, 4, CPB * P], FP32))
        small = ctx.enter_context(nc.psum_tensor("small_setup", [P, 4, CPB * P], FP32))
        loaded = sem("edges_loaded")
        padded = sem("padding_written")
        consts = sem("constants_made")
        dve_step = sem("setup_vector_step")
        floats_ready = sem("floats_ready")
        turned = sem("edges_transposed")
        extremes_ready = sem("extremes_ready")
        extremes_turned = sem("extremes_transposed")
        diagonal_ready = sem("diagonal_ready")
        extremes_spread = sem("extremes_spread")
        hot_ready = sem("digits_ready")
        counted = sem("tiles_counted")
        running_ready = sem("running_ready")
        offsets_done = sem("offsets_done")
        starts_ready = sem("starts_ready")
        descents_ready = sem("descents_ready")
        descents_summed = sem("descents_summed")
        row_loaded = sem("start_row_loaded")
        pads_ready = sem("pads_ready")
        pads_stored = sem("pads_stored")

        loads = []
        arrays = (dram.dst, dram.src, dram.type, dram.w)
        blocks_of = lambda a, lo, n: a[lo:lo + BLOCK * n].rearrange("(b e) -> b e", e=BLOCK)
        line = lambda a, lo, hi: a[lo:hi].rearrange("(o e) -> o e", o=1)
        for n, (buf, arr) in enumerate(zip(raw_i + [raw_f[3]], arrays)):
            loads.append((buf[0:full, :], blocks_of(arr, 0, full)))
            if rest:
                loads.append((buf[full:full + 1, 0:rest], line(arr, full * BLOCK, s.edges)))
            if n:
                if rest:
                    loads.append((buf[full:full + 1, rest:BLOCK], line(arr, 0, BLOCK - rest)))
                done = full + (1 if rest else 0)
                if done < NB:
                    loads.append((buf[done:NB, :], blocks_of(arr, 0, NB - done)))
        after_full = (s.edges - 1) // BLOCK
        after_rest = s.edges - 1 - after_full * BLOCK
        loads.append((next_i[0:after_full, :], blocks_of(dram.dst, 1, after_full)))
        if after_rest:
            loads.append((next_i[after_full:after_full + 1, 0:after_rest],
                          line(dram.dst, 1 + after_full * BLOCK, s.edges)))
        for r, root in enumerate((dram.root1, dram.root2)):
            loads.append((k.root[r][:], root))
        for r, w in enumerate((dram.w1, dram.w2)):
            loads.append((k.wrel[r][:].rearrange("p (r n) -> p r n", r=RELATIONS), w.rearrange("r p n -> p r n")))
        loads.append((raw_m[:], dram.w0))
        for r, b in enumerate((dram.b1, dram.b2)):
            loads.append((bias_f[r][:], b.rearrange("(o n) -> o n", o=1).to_broadcast([3, P])))

        block = ctx.enter_context(nc.Block())

        @block.sync
        def _(sp):
            sp.wait_ge(padded, 2)
            for out, in_ in loads:
                sp.dma_start(out, in_).then_inc(loaded, 16)
            sp.wait_ge(pads_ready, 1)
            sp.dma_start(dram.edge_rows[0:WIDE, :].rearrange("(p c) r -> p (c r)", c=WIDE // P),
                         pads[:, 0:WIDE // P * ROW]).then_inc(pads_stored, 16)
            last = s.first_row + s.blocks * BLOCK
            sp.dma_start(dram.edge_rows[last:last + BLOCK, :].rearrange("(p c) r -> p (c r)", c=CPB),
                         pads[:]).then_inc(pads_stored, 16)
            sp.wait_ge(starts_ready, 1)
            sp.dma_start(dram.starts.rearrange("o (a b) -> (o a) b", b=DIGIT), starts[:]).then_inc(row_loaded, 16)
            sp.wait_ge(row_loaded, 16)
            sp.dma_start(row[:], dram.starts).then_inc(row_loaded, 16)
            sp.wait_ge(row_loaded, 32)
            sp.wait_ge(pads_stored, 32)

        @block.gpsimd
        def _(pool):
            nc.gpsimd.memset(ones[:], 1.0).then_inc(consts, 1)
            nc.gpsimd.iota(k.node[:], pattern=[[1, TPB * P]], base=0, channel_multiplier=0,
                           allow_small_or_imprecise_dtypes=True).then_inc(consts, 1)
            nc.gpsimd.iota(k.minus_base[:], pattern=[[-TPB * P, s.batches]], base=0, channel_multiplier=0,
                           allow_small_or_imprecise_dtypes=True).then_inc(consts, 1)
            pool.wait_ge(consts, 3)
            nc.gpsimd.affine_select(out=k.ident[:], in_=ones[:], compare_op=ALU.is_equal, fill=0.0,
                                    base=0, pattern=[[-1, P]], channel_multiplier=1).then_inc(consts, 1)
            nc.gpsimd.affine_select(out=below[:], in_=ones[0:DIGIT, 0:DIGIT], compare_op=ALU.is_gt, fill=0.0,
                                    base=0, pattern=[[1, DIGIT]], channel_multiplier=-1).then_inc(consts, 1)

        @block.vector
        def _(dve):
            v = nc.vector
            made = [0]

            def link(ins, ready=None):
                made[0] += 1
                ins.then_inc(dve_step, 1)
                dve.wait_ge(dve_step, made[0])
                if ready is not None:
                    dve.sem_inc(ready, 1)

            v.memset(raw_i[0][:], int(NO_NODE)).then_inc(padded, 1)
            v.memset(next_i[:], int(NO_NODE)).then_inc(padded, 1)
            link(v.memset(k.zeros[:], 0.0))
            link(v.memset(k.ones3[:], 1.0))
            link(v.memset(zeros_d[:], 0.0))
            link(v.memset(pads[:], 0.0))
            pad_dst = pads[:].rearrange("p (c r) -> p c r", r=ROW)[:, :, P:P + 1]
            link(v.memset(pad_dst, NO_NODE), pads_ready)
            dve.wait_ge(consts, 5)
            dve.wait_ge(loaded, 16 * len(loads))
            for n in range(3):
                link(v.tensor_copy(raw_f[n][:], raw_i[n][:]), floats_ready if n == 2 else None)
            link(v.tensor_copy(next_f[:], next_i[:]))
            link(v.tensor_tensor(next_f[:], next_f[:], raw_f[0][:], ALU.is_lt))
            link(v.memset(descents[:], 0.0))
            link(v.tensor_reduce(descents[0:NB, :], next_f[:], AX.X, ALU.add), descents_ready)
            col = lambda t: t[:].rearrange("p (b c) -> p c b", c=CPB)
            dve.wait_ge(turned, 1)
            for n, out in enumerate((k.dst_col, k.src_col, type_col, w_col)):
                link(v.tensor_copy(col(out), tp[:, n].rearrange("p (c b) -> p c b", c=CPB)[:, :, 0:NB]))
            link(v.tensor_reduce(extremes[:, 0:1], w_col[:], AX.X, ALU.max))
            link(v.tensor_reduce(extremes[:, 1:2], w_col[:], AX.X, ALU.min))
            link(v.tensor_scalar(extremes[:, 1:2], extremes[:, 1:2], -1.0, None, ALU.mult), extremes_ready)
            dve.wait_ge(extremes_turned, 1)
            link(v.tensor_reduce(ext_t[:], small[0:2, 0, 0:P], AX.X, ALU.max))
            link(v.tensor_scalar(ext_d[:], k.ident[0:2, 0:2], ext_t[:, 0:1], None, ALU.mult), diagonal_ready)
            link(v.tensor_copy(k.w0t[:], small[:, 1, 0:P]))
            dve.wait_ge(extremes_spread, 1)
            link(v.tensor_copy(ext_b[:], small[:, 2, 0:2]))
            link(v.tensor_scalar(span[:, 0:1], ext_b[:, 0:1], ext_b[:, 1:2], EW_EPS, ALU.add, ALU.add))
            link(v.reciprocal(span[:, 1:2], span[:, 0:1]))
            link(v.tensor_scalar(w_col[:], w_col[:], ext_b[:, 1:2], span[:, 1:2], ALU.add, ALU.mult))
            coef = k.coef[:].rearrange("p (q r) -> p q r", r=RELATIONS)
            for r in range(RELATIONS):
                link(v.scalar_tensor_tensor(out=coef[:, :, r], in0=type_col[:], scalar=float(r), in1=w_col[:],
                                            op0=ALU.is_equal, op1=ALU.mult))
            link(v.tensor_copy(dst_int[:], k.dst_col[:]))
            link(v.tensor_scalar(digit_i[0][:], dst_int[:], 12, None, ALU.arith_shift_right))
            link(v.tensor_scalar(digit_i[1][:], dst_int[:], 7, DIGIT - 1, ALU.arith_shift_right, ALU.bitwise_and))
            for i in range(2):
                link(v.tensor_copy(digit_f[i][:], digit_i[i][:]))
            for i in range(2):
                for d in range(DIGIT):
                    ins = v.tensor_scalar(hot[i][:, :, d], digit_f[i][:], float(d), None, ALU.is_equal)
                    if d < DIGIT - 1:
                        made[0] += 1
                        ins.then_inc(dve_step, 1)
                link(ins, hot_ready)
            dve.wait_ge(counted, 1)
            link(v.tensor_copy(counts[:], small[0:DIGIT, 3, 0:DIGIT]))
            link(v.tensor_tensor_scan(running[:], zeros_d[:], counts[:], 0.0, ALU.add, ALU.add), running_ready)
            dve.wait_ge(offsets_done, 1)
            link(v.tensor_tensor(starts[:], running[:], counts[:], ALU.subtract))
            link(v.tensor_scalar(starts[:], starts[:], small[0:DIGIT, 3, 64:65], None, ALU.add), starts_ready)
            dve.wait_ge(descents_summed, 1)
            link(v.tensor_scalar(flag[:, 0:1], small[0:1, 0, 200:201], 0.5, None, ALU.is_gt))
            link(v.tensor_scalar(flag[:, 1:2], flag[:, 0:1], -1.0, 1.0, ALU.mult, ALU.add))
            dve.wait_ge(row_loaded, 32)
            B = s.batches
            per = TPB // PAIRS
            every = lambda first, n: row[:, first:first + s.tiles].rearrange("o (b j) -> o b j", j=n)
            pair_start = every(0, per)[:, :, 0].rearrange("o (b i) -> o b i", i=PAIRS)
            pair_end = every(per, per)[:, :, 0].rearrange("o (b i) -> o b i", i=PAIRS)
            batch_start = every(0, TPB)[:, :, 0]
            batch_end = every(TPB, TPB)[:, :, 0]
            link(v.tensor_tensor(size[:], pair_end, pair_start, ALU.subtract))
            link(v.tensor_reduce(crowd[:], size[:], AX.X, ALU.max))
            link(v.tensor_scalar(wide[:], crowd[:], float(P), flag[:, 0:1], ALU.is_gt, ALU.max))
            link(v.tensor_scalar(crowd[:], crowd[:], float(WIDE), flag[:, 0:1], ALU.is_gt, ALU.max))
            link(v.tensor_scalar(calm[:], crowd[:], -1.0, 1.0, ALU.mult, ALU.add))
            link(v.tensor_tensor(scratch[:], batch_end, batch_start, ALU.subtract))
            link(v.tensor_scalar(scratch[:], scratch[:], float(BLOCK - 1), None, ALU.add))
            link(v.tensor_copy(scratch_i[:], scratch[:]))
            link(v.tensor_scalar(scratch_i[:], scratch_i[:], 9, None, ALU.arith_shift_right))
            link(v.tensor_copy(scratch[:], scratch_i[:]))
            link(v.tensor_tensor(scratch[:], scratch[:], crowd[:], ALU.mult))
            link(v.tensor_scalar(scratch[:], scratch[:], flag[:, 1:2], None, ALU.mult))
            link(v.tensor_scalar(need_f[:], crowd[:], flag[:, 0:1], float(NB), ALU.mult, ALU.mult))
            link(v.tensor_tensor(scratch[:], scratch[:], need_f[:], ALU.add))
            link(v.tensor_tensor(scratch[:], scratch[:], wide[:], ALU.add))
            link(v.memset(k.kind[:], 0))
            link(v.tensor_copy(k.kind[:, 0:s.batches], scratch[:]))
            table = k.table[:].rearrange("o (b j) -> o b j", j=4)
            link(v.tensor_scalar(scratch[:], batch_start, flag[:, 1:2], float(s.first_row), ALU.mult, ALU.add))
            link(v.tensor_copy(table[:, :, 0], scratch[:]))
            link(v.tensor_copy(need_i[:], batch_end))
            link(v.tensor_scalar(need_i[:], need_i[:], 9, None, ALU.arith_shift_right))
            link(v.tensor_copy(scratch[:], need_i[:]))
            link(v.tensor_scalar(need_f[:], crowd[:], flag[:, 0:1], float(NB), ALU.mult, ALU.mult))
            link(v.tensor_scalar(scratch[:], scratch[:], 2.0, float(NB), ALU.add, ALU.min))
            link(v.tensor_tensor(scratch[:], scratch[:], need_f[:], ALU.max))
            link(v.tensor_copy(table[:, :, 1], scratch[:]))
            for i in range(PAIRS):
                link(v.tensor_scalar(scratch[:], pair_start[:, :, i], float(s.first_row), None, ALU.add))
                link(v.tensor_tensor(scratch[:], scratch[:], calm[:], ALU.mult))
                link(v.tensor_copy(table[:, :, 2 + i], scratch[:]))
            for r in range(2):
                link(v.tensor_copy(part[r][0][:], bias_f[r][:]))
                link(v.tensor_tensor(left[r][0][:], bias_f[r][:], part[r][0][:], ALU.subtract))
                link(v.tensor_copy(part[r][1][:], left[r][0][:]))
                link(v.tensor_tensor(left[r][1][:], left[r][0][:], part[r][1][:], ALU.subtract))
                link(v.tensor_copy(part[r][2][:], left[r][1][:]))
                link(v.tensor_scalar(pick[r][0][:], part[r][0][:], k.ident[0:3, 0:1], None, ALU.mult))
                for j in (1, 2):
                    link(v.scalar_tensor_tensor(out=pick[r][j % 2][:], in0=part[r][j][:],
                                                scalar=k.ident[0:3, j:j + 1], in1=pick[r][(j + 1) % 2][:],
                                                op0=ALU.mult, op1=ALU.add))
                for j in range(TPB):
                    link(v.tensor_copy(k.bias[r][:, P * j:P * (j + 1)], pick[r][0][:]))

        @block.tensor
        def _(pe):
            pe.wait_ge(consts, 5)
            pe.wait_ge(floats_ready, 1)
            for n in range(4):
                edges = raw_f[n][:].rearrange("b (p c) -> b c p", c=CPB)
                for c in range(CPB):
                    last = nc.tensor.transpose(tp[:, n, P * c:P * c + NB], edges[:, c, :], k.ident[0:NB, 0:NB])
            last.then_inc(turned, 1)
            pe.wait_ge(extremes_ready, 1)
            nc.tensor.transpose(small[0:2, 0, 0:P], extremes[:], k.ident[:])
            nc.tensor.transpose(small[:, 1, 0:P], raw_m[:], k.ident[:]).then_inc(extremes_turned, 1)
            pe.wait_ge(diagonal_ready, 1)
            nc.tensor.matmul(small[:, 2, 0:2], ones[0:2, :], ext_d[:], start=True, stop=True).then_inc(extremes_spread, 1)
            pe.wait_ge(hot_ready, 2)
            for q in range(NB * CPB):
                last = nc.tensor.matmul(small[0:DIGIT, 3, 0:DIGIT], hot[0][:, q, :], hot[1][:, q, :],
                                        start=(q == 0), stop=(q == NB * CPB - 1))
            last.then_inc(counted, 1)
            pe.wait_ge(running_ready, 1)
            nc.tensor.matmul(small[0:DIGIT, 3, 64:65], below[:], running[:, DIGIT - 1:DIGIT], start=True,
                             stop=True).then_inc(offsets_done, 1)
            pe.wait_ge(descents_ready, 1)
            nc.tensor.matmul(small[0:1, 0, 200:201], ones[:, 0:1], descents[:], start=True,
                             stop=True).then_inc(descents_summed, 1)


class Sums:

    def __init__(self, nc, ctx, sem, s, k, dram, name, transposed):
        self.nc, self.s, self.k, self.rows, self.transposed = nc, s, k, dram.edge_rows, transposed
        sb = lambda n, sh: ctx.enter_context(nc.sbuf_tensor(f"{name}_{n}", sh, FP32))
        self.window = sb("window", [P, UNROLL, PAIRS, WIDE // P, ROW])
        self.ends = sb("ends", [P, 2, TPB, P])
        self.second_ends = sb("second_ends", [P, TPB, P])
        self.step = sb("step", [P, CPB, ROW])
        self.step_ends = sb("step_ends", [P, CPB, TPB, P])
        self.loaded = [sem(f"windows_loaded{i}") for i in range(UNROLL)]
        self.built = sem("ends_built")
        self.added = sem("windows_added")
        self.second_free = sem("second_free")
        self.second_built = sem("second_built")
        self.chunk_free = [sem(f"chunk_free{i}") for i in range(CPB)]
        self.chunk_loaded = [sem(f"chunk_loaded{i}") for i in range(CPB)]
        self.chunk_built = [sem(f"chunk_built{i}") for i in range(CPB)]
        self.kinds = {}

    def kind_of(self, engine, at):
        if at.slot % KINDS == 0:
            _, self.kinds[engine.engine] = self.nc.values_load_multi_w_load_instructions(
                self.k.kind[0:1, bass.ds(at.b, KINDS)], engines=[engine.engine], min_val=0, max_val=self.s.blocks + 1,
                skip_runtime_bounds_check_because="worked out on the chip from counts of the edges")
        return self.kinds[engine.engine][at.slot % KINDS]

    def load(self, sp, at, stored):
        _, (first, need, *starts) = self.nc.values_load_multi_w_load_instructions(
            self.k.table[0:1, bass.ds(at.b * 4, 4)], engines=[sp.engine], min_val=0, max_val=self.s.rows - BLOCK,
            skip_runtime_bounds_check_because="counts of edges behind the first padding, which a block of padding follows")
        kind = self.kind_of(sp, at)
        if stored is not None:
            sp.wait_ge(stored, self.nc.s_assert_within(need, 1, self.s.blocks))
            sp.sem_inc(self.k.passed, 1)
        if at.at_least(UNROLL):
            sp.wait_ge(self.added, at.b - UNROLL + 1)
        sp.sem_inc(self.k.passed, 1)
        with sp.If(kind > 0):
            for i in range(PAIRS):
                sp.dma_start(self.window[:, at.slot, i],
                             self.rows[bass.ds(starts[i], WIDE), :].rearrange("(c p) r -> p c r", p=P)
                             ).then_inc(self.loaded[at.slot], 16)
            with sp.If(kind > 1):
                with sp.Fori(1, kind) as x:
                    for c in range(CPB):
                        row = self.nc.s_assert_within(
                            first + (x - 1) * BLOCK + c * P, 0, self.s.rows - P,
                            skip_runtime_bounds_check_because="a block of padding follows the batch's rows")
                        sp.wait_ge(self.chunk_free[c], 1)
                        sp.sem_clear(self.chunk_free[c])
                        sp.dma_start(self.step[:, c], self.rows[bass.ds(row, P), :]).then_inc(self.chunk_loaded[c], 16)
        with sp.Else():
            for i in range(PAIRS):
                sp.dma_start(self.window[:, at.slot, i, 0], self.rows[bass.ds(starts[i], P), :]
                             ).then_inc(self.loaded[at.slot], 16)

    def begin(self, dve):
        dve.sem_inc(self.second_free, 1)
        for c in range(CPB):
            dve.sem_inc(self.chunk_free[c], 1)

    def match(self, at, ends, destinations, tiles):
        split = lambda t: t[:, tiles.start * P:tiles.stop * P]
        return self.nc.vector.tensor_scalar(split(ends.rearrange("p t n -> p (t n)")), split(self.k.node[:]),
                                            destinations, self.k.minus_base[:, bass.ds(at.b, 1)], ALU.subtract,
                                            ALU.is_equal)

    def build_steps(self, dve, at):
        kind = self.kind_of(dve, at)
        with dve.If(kind > 0):
            with dve.If(kind > 1):
                with dve.Fori(1, kind) as x:
                    for c in range(CPB):
                        dve.wait_ge(self.chunk_loaded[c], 16)
                        dve.sem_clear(self.chunk_loaded[c])
                        self.match(at, self.step_ends[:, c], self.step[:, c, P:P + 1],
                                   range(TPB)).then_inc(self.chunk_built[c], 1)
            dve.wait_ge(self.loaded[at.slot], (at.turn + 1) * 16 * PAIRS)
            dve.sem_inc(self.k.passed, 1)
            dve.wait_ge(self.second_free, 1)
            dve.sem_clear(self.second_free)
            for i in range(PAIRS):
                last = self.match(at, self.second_ends[:], self.window[:, at.slot, i, 1, P:P + 1], TILES_OF_PAIR[i])
            last.then_inc(self.second_built, 1)

    def build(self, dve, at):
        dve.wait_ge(self.loaded[at.slot], (at.turn + 1) * 16 * PAIRS)
        if at.at_least(2):
            dve.wait_ge(self.added, at.b - 1)
        for i in range(PAIRS):
            last = self.match(at, self.ends[:, at.slot % 2], self.window[:, at.slot, i, 0, P:P + 1], TILES_OF_PAIR[i])
        last.then_inc(self.built, 1)

    def products(self, bank, ends, rows, tiles):
        if self.transposed:
            return self.nc.tensor.matmul(bank[:, tiles.start:tiles.stop].rearrange("p t n -> p (t n)"), rows,
                                         ends[:, tiles.start:tiles.stop].rearrange("p t n -> p (t n)"), start=False,
                                         stop=True, skip_group_check=True)
        for j in tiles:
            last = self.nc.tensor.matmul(bank[:, j], ends[:, j], rows, start=False, stop=True, skip_group_check=True)
        return last

    def add(self, pe, at, bank):
        kind = self.kind_of(pe, at)
        with pe.If(kind > 0):
            with pe.If(kind > 1):
                with pe.Fori(1, kind) as x:
                    for c in range(CPB):
                        pe.wait_ge(self.chunk_built[c], 1)
                        pe.sem_clear(self.chunk_built[c])
                        self.products(bank, self.step_ends[:, c], self.step[:, c, 0:P],
                                      range(TPB)).then_inc(self.chunk_free[c], 1)
            pe.wait_ge(self.second_built, 1)
            pe.sem_clear(self.second_built)
            for i in range(PAIRS):
                last = self.products(bank, self.second_ends, self.window[:, at.slot, i, 1, 0:P], TILES_OF_PAIR[i])
            last.then_inc(self.second_free, 1)
        pe.wait_ge(self.built, at.b + 1)
        for i in range(PAIRS):
            last = self.products(bank, self.ends[:, at.slot % 2], self.window[:, at.slot, i, 0, 0:P], TILES_OF_PAIR[i])
        last.then_inc(self.added, 1)


def gathered_blocks(s, phase, slot, turns):
    return (turns + phase * len(range(slot, s.blocks, RING))) * (16 * CPB)


def stage_index(nc, k, at, index, staged):
    nc.gpsimd.tensor_copy(index[:, at.slot, :], k.src_col[:, bass.ds(at.b * CPB, CPB)]).then_inc(staged, 1)


def gather_block(nc, pool, k, table, ring, at, index, staged, gathered):
    pool.wait_ge(staged, at.b + 1)
    pool.sem_inc(k.passed, 1)
    for c in range(CPB):
        nc.gpsimd.indirect_dma_start(
            out=ring[:, at.slot, c, 0:P], out_offset=None, in_=table,
            in_offset=bass.IndirectOffsetOnAxis(ap=index[:, at.slot, c:c + 1], axis=0)).then_inc(gathered[at.slot], 16)


def block_rows(dram, s, at):
    return dram.edge_rows[bass.ds(at.b * BLOCK + s.first_row, BLOCK), :].rearrange("(p c) r -> p (c r)", c=CPB)


class Norm:

    SLOTS = 4

    def __init__(self, nc, ctx, sem, name):
        self.nc = nc
        sb = lambda n, sh: ctx.enter_context(nc.sbuf_tensor(f"{name}_{n}", sh, FP32))
        self.v = sb("to_norm", [P, self.SLOTS, TPB, P])
        self.stats = sb("bn_stats", [P, self.SLOTS, TPB, nc.vector.BN_STATS_DIM])
        self.moments = sb("moments", [P, self.SLOTS, TPB, nc.vector.BN_AGGR_DIM])
        self.std = sb("std", [P, self.SLOTS, TPB])
        self.rstd = sb("rstd", [P, self.SLOTS, TPB])
        self.shift = sb("shift", [P, self.SLOTS, TPB])
        self.eps = sb("eps", [P, 1])
        self.out = sb("normed", [P, UNROLL, TPB, P])
        self.summed = sem("summed")
        self.stats_done = sem("stats_done")
        self.moments_begun = sem("moments_begun")
        self.moments_done = sem("moments_done")
        self.std_done = sem("std_done")
        self.rstd_done = sem("rstd_done")
        self.shift_done = sem("shift_done")
        self.normed = sem("normed")
        self.eps_made = sem("eps_made")

    def constants(self):
        self.nc.vector.memset(self.eps[:], LN_EPS).then_inc(self.eps_made, 1)

    def sum(self, dve, at, update, rows):
        if at.at_least(self.SLOTS):
            dve.wait_ge(self.normed, (at.b - self.SLOTS + 1) * TPB)
        self.nc.vector.tensor_tensor(self.v[:, at.slot % self.SLOTS], update, rows, ALU.add).then_inc(self.summed, 1)

    def statistics(self, dve, at):
        h = at.slot % self.SLOTS
        dve.wait_ge(self.summed, at.b + 1)
        for j in range(TPB):
            last = self.nc.vector.bn_stats(self.stats[:, h, j, :], self.v[:, h, j, :])
        last.then_inc(self.stats_done, 1)

    def aggregate(self, dve, at):
        h = at.slot % self.SLOTS
        dve.wait_ge(self.stats_done, at.b + 1)
        dve.sem_inc(self.moments_begun, 1)
        for j in range(TPB):
            last = self.nc.vector.bn_aggr(self.moments[:, h, j, :], self.stats[:, h, j, :])
        last.then_inc(self.moments_done, 1)

    def deviation(self, act, at):
        h = at.slot % self.SLOTS
        act.wait_ge(self.moments_done, at.b + 1)
        self.nc.scalar.activation(self.std[:, h, :], self.moments[:, h, :, 1], ACT.Sqrt,
                                  bias=self.eps[:]).then_inc(self.std_done, 1)

    def invert(self, dve, at):
        h = at.slot % self.SLOTS
        dve.wait_ge(self.std_done, at.b + 1)
        self.nc.vector.reciprocal(self.rstd[:, h, :], self.std[:, h, :]).then_inc(self.rstd_done, 1)

    def offset(self, dve, at):
        h = at.slot % self.SLOTS
        dve.wait_ge(self.rstd_done, at.b + 1)
        self.nc.vector.scalar_tensor_tensor(out=self.shift[:, h, :], in0=self.moments[:, h, :, 0], scalar=-1.0,
                                            in1=self.rstd[:, h, :], op0=ALU.mult,
                                            op1=ALU.mult).then_inc(self.shift_done, 1)

    def apply(self, act, at, stored):
        h = at.slot % self.SLOTS
        act.wait_ge(self.shift_done, at.b + 1)
        if at.at_least(UNROLL):
            act.wait_ge(stored[at.slot // PAIR], at.turn * 16)
        for j in range(TPB):
            self.nc.scalar.activation(self.out[:, at.slot, j, :], self.v[:, h, j, :], ACT.Identity,
                                      bias=self.shift[:, h, j:j + 1],
                                      scale=self.rstd[:, h, j:j + 1]).then_inc(self.normed, 1)


def pair_rows(array, at):
    return array[bass.ds(at.b * (TPB * P), PAIR * TPB * P), :].rearrange("(t p) f -> p t f", p=P)


def pair_slots(ring, at):
    return ring[:, at.slot:at.slot + PAIR].rearrange("p b t f -> p (b t) f")


def is_last(s, at):
    return isinstance(at.b, int) and at.b == s.batches - PAIR and s.tail < PAIR * TPB * P


def load_pair(sp, s, k, array, at, ring, loaded, zeroed, padded=True):
    out = pair_slots(ring, at)
    if padded or not is_last(s, at):
        sp.dma_start(out, pair_rows(array, at)).then_inc(loaded[at.slot // PAIR], 16)
        return
    whole, rest = divmod(s.tail, P)
    base = at.b * TPB * P
    tiles = PAIR * TPB
    for first in range(whole, tiles, TPB):
        n = min(TPB, tiles - first)
        sp.dma_start(out[:, first:first + n], k.zeros[:, 0:n * P].rearrange("p (t f) -> p t f", f=P)
                     ).then_inc(zeroed, 16)
    done = 16 * len(range(whole, tiles, TPB))
    sp.wait_ge(zeroed, done)
    parts = []
    if whole:
        parts.append((out[:, 0:whole], array[base:base + whole * P, :].rearrange("(t p) f -> p t f", p=P)))
    if rest:
        parts.append((out[0:rest, whole], array[base + whole * P:s.nodes, :]))
    for o, i in parts[:-1]:
        sp.dma_start(o, i).then_inc(zeroed, 16)
        sp.wait_ge(zeroed, done + 16)
    sp.dma_start(*parts[-1]).then_inc(loaded[at.slot // PAIR], 16)


def store_pair(sp, s, array, at, ring, stored, padded):
    src = pair_slots(ring, at)
    if padded or not is_last(s, at):
        sp.dma_start(pair_rows(array, at), src).then_inc(stored[at.slot // PAIR], 16)
        return
    whole, rest = divmod(s.tail, P)
    base = at.b * TPB * P
    if whole:
        sp.dma_start(array[base:base + whole * P, :].rearrange("(t p) f -> p t f", p=P),
                     src[:, 0:whole]).then_inc(stored[at.slot // PAIR], 16)
    if rest:
        sp.dma_start(array[base + whole * P:s.nodes, :], src[0:rest, whole]).then_inc(stored[at.slot // PAIR], 16)


def wait_stored(sp, s, stored, padded):
    pieces = 1 if padded or s.tail == PAIR * TPB * P else (s.tail >= P) + (s.tail % P > 0)
    pairs = s.batches // PAIR
    for slot in range(UNROLL // PAIR):
        n = len(range(slot, pairs, UNROLL // PAIR))
        last = slot == (pairs - 1) % (UNROLL // PAIR)
        sp.wait_ge(stored[slot], 16 * (n + (pieces - 1 if last else 0)))


def first_phase(nc, s, k, dram):
    with ExitStack() as ctx:
        sem = ctx.enter_context(phase_semaphores(nc, "l0_"))
        sums = Sums(nc, ctx, sem, s, k, dram, "l0", True)
        norm = Norm(nc, ctx, sem, "l0")
        sb = lambda n, sh, dt=FP32: ctx.enter_context(nc.sbuf_tensor(n, sh, dt))
        ps = lambda n: ctx.enter_context(nc.psum_tensor(n, [P, TPB, P], FP32))
        x_ring = sb("x_ring", [P, UNROLL, TPB, P])
        zt = sb("zt", [P, 2, TPB, P])
        index = sb("l0_index", [P, RING, CPB], I32)
        gather_ring = sb("gather_ring", [P, RING, CPB, ROW])
        zt_ps = [ps(f"zt_ps{i}") for i in range(2)]
        update_ps = [ps(f"update{i}") for i in range(2)]
        x_loaded = [sem(f"x_loaded{i}") for i in range(UNROLL // PAIR)]
        x_zeroed = sem("x_zeroed")
        stored = [sem(f"x1_stored{i}") for i in range(UNROLL // PAIR)]
        gathered, rows_stored = k.gathered, k.rows_stored
        landed = lambda at, turns: gathered_blocks(s, 0, at.slot, turns)
        staged = sem("l0_index_staged")
        blocks_stored = sem("l0_blocks_stored")
        marked = sem("l0_marked")
        zt_done = sem("zt_copied")
        update_done = sem("update_done")
        B = s.batches
        block = ctx.enter_context(nc.Block())

        @block.sync
        def _(sp):
            def body(at):
                if at.within(B):
                    if at.slot % PAIR == 0:
                        if at.at_least(UNROLL):
                            sp.wait_ge(norm.summed, at.b - UNROLL + PAIR)
                            sp.sem_inc(k.passed, 1)
                        load_pair(sp, s, k, dram.x, at, x_ring, x_loaded, x_zeroed, False)
                    sums.load(sp, at, blocks_stored)

            each(sp, body, B, UNROLL)

        @block.gpsimd
        def _(pool):
            nc.gpsimd.memset(gather_ring[:], 0.0).then_inc(marked, 1)
            pool.wait_ge(marked, 1)

            def body(at):
                store = at.back(1)
                if store.within(s.blocks):
                    pool.wait_ge(marked, store.b + 2)
                    pool.sem_inc(k.passed, 1)
                    pool.wait_ge(gathered[store.slot], landed(store, store.turn + 1))
                    pool.dma_start(block_rows(dram, s, store), gather_ring[:, store.slot].rearrange("p c r -> p (c r)")
                                   ).then_inc(rows_stored[store.slot], 16)
                told = at.back(3)
                if told.within(s.blocks):
                    pool.wait_ge(rows_stored[told.slot], (told.turn + 1) * 16)
                    pool.sem_inc(blocks_stored, 1)
                after = at.ahead(1)
                if after.within(s.blocks):
                    if after.at_least(RING):
                        pool.wait_ge(gathered[after.slot], landed(after, after.turn))
                    stage_index(nc, k, after, index, staged)
                if at.within(s.blocks):
                    if at.at_least(RING):
                        pool.wait_ge(rows_stored[at.slot], at.turn * 16)
                    nc.gpsimd.tensor_copy(gather_ring[:, at.slot, :, P],
                                          k.dst_col[:, bass.ds(at.b * CPB, CPB)]).then_inc(marked, 1)
                    gather_block(nc, pool, k, dram.x, gather_ring, at, index, staged, gathered)

            stage_index(nc, k, At(0, 0, 0, RING), index, staged)
            each(pool, body, s.blocks, RING, drain=3)

        @block.vector
        def _(dve):
            norm.constants()
            sums.begin(dve)

            def body(at):
                two, three, four = at.back(2), at.back(3), at.back(4)
                if at.within(B):
                    sums.build_steps(dve, at)
                    sums.build(dve, at)
                if three.within(B):
                    norm.aggregate(dve, three)
                if four.within(B):
                    norm.invert(dve, four)
                if two.within(B):
                    dve.wait_ge(update_done, two.b + 1)
                    norm.sum(dve, two, update_ps[two.slot % 2][:], x_ring[:, two.slot])
                if four.within(B):
                    norm.offset(dve, four)
                if two.within(B):
                    norm.statistics(dve, two)

            each(dve, body, B, UNROLL, drain=4)

        @block.tensor
        def _(pe):
            def body(at):
                if at.within(B):
                    bank = zt_ps[at.slot % 2]
                    pe.wait_ge(x_loaded[at.slot // PAIR], (at.turn + 1) * 16)
                    if at.at_least(2):
                        pe.wait_ge(zt_done, at.b - 1)
                    for j in range(TPB):
                        nc.tensor.matmul(bank[:, j], x_ring[:, at.slot, j], k.ident[:], start=(j == 0), stop=True,
                                         skip_group_check=True)
                    sums.add(pe, at, bank)
                prev = at.back(1)
                if prev.within(B):
                    pe.wait_ge(zt_done, prev.b + 1)
                    if prev.at_least(2):
                        pe.wait_ge(norm.summed, prev.b - 1)
                    for j in range(TPB):
                        last = nc.tensor.matmul(update_ps[prev.slot % 2][:, j], zt[:, prev.slot % 2, j], k.w0t[:],
                                                start=True, stop=True)
                    last.then_inc(update_done, 1)

            each(pe, body, B, UNROLL, drain=1)

        @block.scalar
        def _(act):
            act.wait_ge(norm.eps_made, 1)

            def body(at):
                prev, three, four, out = at.back(1), at.back(3), at.back(4), at.back(6)
                if prev.within(B):
                    act.wait_ge(sums.added, prev.b + 1)
                    if prev.at_least(2):
                        act.wait_ge(update_done, prev.b - 1)
                    nc.scalar.copy(zt[:, prev.slot % 2], zt_ps[prev.slot % 2][:]).then_inc(zt_done, 1)
                if three.within(B):
                    norm.deviation(act, three)
                if four.within(B):
                    norm.apply(act, four, stored)
                if out.within(B) and out.slot % PAIR == 0:
                    act.wait_ge(norm.normed, (out.b + PAIR) * TPB)
                    act.sem_inc(k.passed, 1)
                    store_pair(act, s, dram.x1, out, norm.out, stored, True)

            each(act, body, B, UNROLL, drain=5)
            wait_stored(act, s, stored, True)


def message_phase(nc, s, k, dram, layer, table):
    name = f"m{layer}"
    with ExitStack() as ctx:
        sem = ctx.enter_context(phase_semaphores(nc, f"{name}_"))
        sb = lambda n, sh, dt=FP32: ctx.enter_context(nc.sbuf_tensor(f"{name}_{n}", sh, dt))
        ring = sb("rows_ring", [P, RING, CPB, P])
        index = sb("index", [P, RING, CPB], I32)
        rows_t = sb("rows_t", [P, 2, P])
        partial = sb("partial", [P, CPB, 3, P])
        messages = sb("messages", [P, RING, CPB, ROW])
        turned_ps = ctx.enter_context(nc.psum_tensor(f"{name}_turned_ps", [P, 2, 4 * P], FP32))
        product_ps = ctx.enter_context(nc.psum_tensor(f"{name}_product_ps", [P, CPB, 4 * P], FP32))
        gathered = k.gathered
        landed = lambda at, turns: gathered_blocks(s, 1 + layer, at.slot, turns)
        stored = [sem(f"stored{i}") for i in range(RING)]
        staged = sem("index_staged")
        turned = sem("turned")
        rows_t_done = sem("rows_t_copied")
        product_done = sem("product_done")
        part0_done = sem("part0_done")
        added = sem("parts_added")
        message_done = sem("message_done")
        cleared = sem("cleared")
        marked = sem("marked")
        wrel = k.wrel[layer]
        B = s.blocks
        coef = lambda c, r: k.coef[:, bass.ds(c * RELATIONS + r, 1)]
        block = ctx.enter_context(nc.Block())

        @block.gpsimd
        def _(pool):
            def body(at):
                after = at.ahead(1)
                if after.within(B):
                    if after.at_least(RING):
                        pool.wait_ge(gathered[after.slot], landed(after, after.turn))
                    stage_index(nc, k, after, index, staged)
                if at.at_least(RING):
                    pool.wait_ge(turned, (at.b - RING + 1) * CPB)
                    pool.sem_inc(k.passed, 1)
                gather_block(nc, pool, k, table, ring, at, index, staged, gathered)

            stage_index(nc, k, At(0, 0, 0, RING), index, staged)
            each(pool, body, B, RING)

        @block.tensor
        def _(pe):
            def turn(at, i):
                c = at.b * CPB + i
                if i == 0:
                    pe.wait_ge(gathered[at.slot], landed(at, at.turn + 1))
                if at.at_least(1) or i >= 2:
                    pe.wait_ge(rows_t_done, c - 1)
                nc.tensor.transpose(turned_ps[:, i % 2, 0:P], ring[:, at.slot, i],
                                    k.ident[:]).then_inc(turned, 1)

            def body(at):
                for i in range(CPB):
                    c = at.b * CPB + i
                    if i < CPB - 1:
                        turn(at, i + 1)
                    elif at.ahead(1).within(B):
                        turn(at.ahead(1), 0)
                    pe.wait_ge(rows_t_done, c + 1)
                    if at.at_least(1):
                        pe.wait_ge(message_done, c - CPB + 1)
                    nc.tensor.matmul(product_ps[:, i], rows_t[:, i % 2], wrel[:], start=True,
                                     stop=True).then_inc(product_done, 1)

            turn(At(0, 0, 0, RING), 0)
            each(pe, body, B, RING)

        @block.scalar
        def _(act):
            def copy_rows(c, i):
                act.wait_ge(turned, c + 1)
                if not isinstance(c, int) or c >= 2:
                    act.wait_ge(product_done, c - 1)
                nc.scalar.copy(rows_t[:, i % 2], turned_ps[:, i % 2, 0:P]).then_inc(rows_t_done, 1)

            def body(at):
                for i in range(CPB):
                    c = at.b * CPB + i
                    last = isinstance(at.b, int) and at.b == B - 1 and i == CPB - 1
                    if not last:
                        copy_rows(c + 1, i + 1)
                    act.wait_ge(product_done, c + 1)
                    nc.scalar.activation(partial[:, i, 0], product_ps[:, i, 0:P], ACT.Copy,
                                         scale=coef(c, 0)).then_inc(part0_done, 1)

            copy_rows(0, 0)
            each(act, body, B, RING)

        @block.vector
        def _(dve):
            nc.vector.memset(messages[:], 0.0).then_inc(cleared, 1)
            dve.wait_ge(cleared, 1)

            def add_part(at, i, r, out):
                return nc.vector.scalar_tensor_tensor(
                    out=out, in0=product_ps[:, i, r * P:(r + 1) * P], scalar=coef(at.b * CPB + i, r),
                    in1=partial[:, i, r - 1], op0=ALU.mult, op1=ALU.add)

            def body(at):
                for i in range(0, CPB, 2):
                    c = at.b * CPB + i
                    dve.wait_ge(part0_done, c + 2)
                    if at.at_least(1):
                        dve.sem_inc(k.passed, 1)
                    for j in range(2):
                        add_part(at, i + j, 1, partial[:, i + j, 1]).then_inc(added, 1)
                    for j in range(2):
                        dve.wait_ge(added, 2 * c + 1 + j)
                        add_part(at, i + j, 2, partial[:, i + j, 2]).then_inc(added, 1)
                    if i == 0:
                        if at.at_least(RING):
                            dve.wait_ge(stored[at.slot], at.turn * 16)
                        nc.vector.tensor_copy(messages[:, at.slot, :, P],
                                              k.dst_col[:, bass.ds(at.b * CPB, CPB)]).then_inc(marked, 1)
                    for j in range(2):
                        dve.wait_ge(added, 2 * c + 3 + j)
                        add_part(at, i + j, 3, messages[:, at.slot, i + j, 0:P]).then_inc(message_done, 1)

            each(dve, body, B, RING)

        @block.sync
        def _(sp):
            def body(at):
                sp.wait_ge(marked, at.b + 1)
                sp.sem_inc(k.passed, 1)
                sp.wait_ge(message_done, (at.b + 1) * CPB)
                sp.sem_inc(k.passed, 1)
                sp.dma_start(block_rows(dram, s, at),
                             messages[:, at.slot].rearrange("p c r -> p (c r)")).then_inc(stored[at.slot], 16)

            each(sp, body, B, RING)
            for slot in range(RING):
                sp.wait_ge(stored[slot], 16 * len(range(slot, B, RING)))


def conv_phase(nc, s, k, dram, layer, table, out):
    name = f"c{layer}"
    normed = layer == 1
    with ExitStack() as ctx:
        sem = ctx.enter_context(phase_semaphores(nc, f"{name}_"))
        sums = Sums(nc, ctx, sem, s, k, dram, name, False)
        norm = Norm(nc, ctx, sem, name) if normed else None
        sb = lambda n, sh, dt=FP32: ctx.enter_context(nc.sbuf_tensor(f"{name}_{n}", sh, dt))
        ps = lambda n: ctx.enter_context(nc.psum_tensor(f"{name}_{n}", [P, TPB, P], FP32))
        rows = sb("rows", [P, UNROLL, TPB, P])
        residual = sb("residual", [P, UNROLL, TPB, P]) if normed else None
        rows_t = sb("rows_t", [P, 2, TPB, P])
        relu = None if normed else sb("relu", [P, UNROLL, TPB, P])
        rows_t_ps = [ps(f"rows_t_ps{i}") for i in range(2)]
        sums_ps = [ps(f"sums{i}") for i in range(2)]
        rows_loaded = [sem(f"rows_loaded{i}") for i in range(UNROLL // PAIR)]
        residual_loaded = [sem(f"residual_loaded{i}") for i in range(UNROLL // PAIR)]
        stored = [sem(f"stored{i}") for i in range(UNROLL // PAIR)]
        turned = sem("rows_turned")
        rows_t_done = sem("rows_t_copied")
        own_done = sem("own_product_done")
        relu_done = sem("relu_done")
        B = s.batches
        block = ctx.enter_context(nc.Block())
        finished = (lambda b: (norm.summed, b + 1)) if normed else (lambda b: (relu_done, b + 1))

        @block.sync
        def _(sp):
            def body(at):
                if at.within(B):
                    if at.slot % PAIR == 0:
                        if at.at_least(UNROLL):
                            sp.wait_ge(turned, at.b - UNROLL + PAIR)
                            sp.sem_inc(k.passed, 1)
                        load_pair(sp, s, k, table, at, rows, rows_loaded, None)
                        if normed:
                            if at.at_least(UNROLL):
                                sp.wait_ge(norm.summed, at.b - UNROLL + PAIR)
                                sp.sem_inc(k.passed, 1)
                            load_pair(sp, s, k, dram.x1, at, residual, residual_loaded, None)
                    sums.load(sp, at, None)

            each(sp, body, B, UNROLL)

        @block.vector
        def _(dve):
            if normed:
                norm.constants()
            sums.begin(dve)

            def body(at):
                prev, two, three = at.back(1), at.back(2), at.back(3)
                if at.within(B):
                    sums.build_steps(dve, at)
                    sums.build(dve, at)
                if normed and two.within(B):
                    norm.aggregate(dve, two)
                if not normed:
                    return
                if three.within(B):
                    norm.invert(dve, three)
                if prev.within(B):
                    dve.wait_ge(own_done, prev.b + 1)
                    dve.wait_ge(residual_loaded[prev.slot // PAIR], (prev.turn + 1) * 16)
                    norm.sum(dve, prev, sums_ps[prev.slot % 2][:], residual[:, prev.slot])
                if three.within(B):
                    norm.offset(dve, three)
                if prev.within(B):
                    norm.statistics(dve, prev)

            each(dve, body, B, UNROLL, drain=3 if normed else 0)

        @block.tensor
        def _(pe):
            def turn(at):
                pe.wait_ge(rows_loaded[at.slot // PAIR], (at.turn + 1) * 16)
                if at.at_least(2):
                    pe.wait_ge(rows_t_done, at.b - 1)
                for j in range(TPB):
                    last = nc.tensor.transpose(rows_t_ps[at.slot % 2][:, j], rows[:, at.slot, j], k.ident[:])
                last.then_inc(turned, 1)

            def body(at):
                bank = sums_ps[at.slot % 2]
                if at.at_least(2):
                    sem_, n = finished(at.b - 2)
                    pe.wait_ge(sem_, n)
                nc.tensor.matmul(bank[:].rearrange("p t f -> p (t f)"), k.ones3[:], k.bias[layer][:], start=True,
                                 stop=True, skip_group_check=True)
                sums.add(pe, at, bank)
                if at.ahead(1).within(B):
                    turn(at.ahead(1))
                pe.wait_ge(rows_t_done, at.b + 1)
                for j in range(TPB):
                    last = nc.tensor.matmul(bank[:, j], rows_t[:, at.slot % 2, j], k.root[layer][:], start=False,
                                            stop=True, skip_group_check=True)
                last.then_inc(own_done, 1)

            turn(At(0, 0, 0, UNROLL))
            each(pe, body, B, UNROLL)

        @block.scalar
        def _(act):
            if normed:
                act.wait_ge(norm.eps_made, 1)

            def body(at):
                if at.within(B):
                    act.wait_ge(turned, at.b + 1)
                    if at.at_least(2):
                        act.wait_ge(own_done, at.b - 1)
                    nc.scalar.copy(rows_t[:, at.slot % 2], rows_t_ps[at.slot % 2][:]).then_inc(rows_t_done, 1)
                prev, two, three = at.back(1), at.back(2), at.back(3)
                if normed and two.within(B):
                    norm.deviation(act, two)
                if normed and three.within(B):
                    norm.apply(act, three, stored)
                if not normed and prev.within(B):
                    act.wait_ge(own_done, prev.b + 1)
                    if prev.at_least(UNROLL):
                        act.wait_ge(stored[prev.slot // PAIR], prev.turn * 16)
                    nc.scalar.activation(relu[:, prev.slot], sums_ps[prev.slot % 2][:], ACT.Relu).then_inc(relu_done, 1)
                done = at.back(lag)
                if done.within(B) and done.slot % PAIR == 0:
                    if normed:
                        act.wait_ge(norm.normed, (done.b + PAIR) * TPB)
                    else:
                        act.wait_ge(relu_done, done.b + PAIR)
                    act.sem_inc(k.passed, 1)
                    store_pair(act, s, out, done, norm.out if normed else relu, stored, not normed)

            lag = 6 if normed else 4
            each(act, body, B, UNROLL, drain=lag - PAIR + 1)
            wait_stored(act, s, stored, not normed)


class Named:
    pass


def build_program(nc, x, src, dst, edge_type, weight, w0, w1, root1, b1, w2, root2, b2, out):
    s = Shapes(x.shape[0], src.shape[0])
    dram = Named()
    dram.x, dram.src, dram.dst, dram.type, dram.w, dram.w0 = x, src, dst, edge_type, weight, w0
    dram.w1, dram.root1, dram.b1, dram.w2, dram.root2, dram.b2, dram.out = w1, root1, b1, w2, root2, b2, out
    rows = s.batches * TPB * P
    dram.x1 = nc.dram_tensor("x1_rows", (rows, P), FP32).ap()
    dram.h1 = nc.dram_tensor("h1_rows", (rows, P), FP32).ap()
    dram.edge_rows = nc.dram_tensor("edge_rows", (s.rows, ROW), FP32).ap()
    dram.starts = nc.dram_tensor("tile_starts", (1, DIGIT * DIGIT), FP32).ap()
    with ExitStack() as ctx:
        k = Named()
        sb = lambda n, sh, dt=FP32: ctx.enter_context(nc.sbuf_tensor(n, sh, dt))
        k.node = sb("node_numbers", [P, TPB * P])
        k.minus_base = sb("minus_batch_base", [P, s.batches])
        k.ident = sb("identity", [P, P])
        k.zeros = sb("zeros", [P, TPB * P])
        k.ones3 = sb("ones3", [3, P], BF16)
        k.dst_col = sb("dst_col", [P, s.blocks * CPB])
        k.src_col = sb("src_col", [P, s.blocks * CPB], I32)
        k.coef = sb("coef", [P, s.blocks * CPB * RELATIONS])
        k.kind = sb("batch_kind", [1, s.batches + KINDS], I32)
        k.table = sb("batch_table", [1, s.batches * 4], I32)
        k.w0t = sb("w0t", [P, P])
        k.root = [sb(f"root{i}", [P, P]) for i in range(2)]
        k.wrel = [sb(f"wrel{i}", [P, RELATIONS * P]) for i in range(2)]
        k.bias = [sb(f"bias{i}", [3, TPB * P], BF16) for i in range(2)]
        k.gathered = [ctx.enter_context(nc.semaphore(f"gathered{i}")) for i in range(RING)]
        k.rows_stored = [ctx.enter_context(nc.semaphore(f"rows_stored{i}")) for i in range(RING)]
        k.passed = ctx.enter_context(nc.semaphore("waits_passed"))
        setup_phase(nc, s, k, dram)
        first_phase(nc, s, k, dram)
        message_phase(nc, s, k, dram, 0, dram.x1)
        conv_phase(nc, s, k, dram, 0, dram.x1, dram.h1)
        message_phase(nc, s, k, dram, 1, dram.h1)
        conv_phase(nc, s, k, dram, 1, dram.h1, dram.out)


_INS = ['x', 'src', 'dst', 'edge_type_4', 'edge_weight', 'L0_gnn_W', 'L1_gnn_W1', 'L1_gnn_root1', 'L1_gnn_b1',
        'L1_gnn_W2', 'L1_gnn_root2', 'L1_gnn_b2']


def kernel(**inputs):
    import numpy as _np
    import concourse.bacc as _bacc
    from concourse import mybir as _mybir
    from concourse.bass_utils import run_bass_kernel_spmd as _run

    nc = _bacc.Bacc("TRN2", target_bir_lowering=False, num_devices=1)
    arrays, args = {}, []
    for name in _INS:
        a = _np.ascontiguousarray(inputs[name])
        arrays[f"in_{name}"] = a
        args.append(nc.dram_tensor(f"in_{name}", a.shape, _mybir.dt.from_np(a.dtype), kind="ExternalInput").ap())
    shape = inputs['x'].shape
    args.append(nc.dram_tensor("out_rows", tuple(shape), FP32, kind="ExternalOutput").ap())
    build_program(nc, *args)
    r = _run(nc, [arrays], core_ids=[0])
    return r.results[0]["out_rows"]
```

```python
from contextlib import ExitStack, contextmanager

import concourse.bass as bass
from concourse import mybir

FP32 = mybir.dt.float32
BF16 = mybir.dt.bfloat16
I32 = mybir.dt.int32
ALU = mybir.AluOpType
ACT = mybir.ActivationFunctionType
AX = mybir.AxisListType

P = 128
TPB = 4
UNROLL = 8
PAIR = 2
KINDS = 4
PAIRS = 2
TILES_OF_PAIR = [range(0, 2), range(2, 4)]
CPB = 4
WIDE = 2 * P
BLOCK = CPB * P
RING = 4
RELATIONS = 4
ROW = P + 4
DIGIT = 32
NO_NODE = float(1 << 20)
LN_EPS = 1e-5
EW_EPS = 1e-8


class Shapes:

    def __init__(self, nodes, edges):
        self.nodes, self.edges = nodes, edges
        self.batches = -(-nodes // (P * TPB * PAIR)) * PAIR
        self.tiles = self.batches * TPB
        self.tail = nodes - (self.batches - PAIR) * TPB * P
        assert 0 < self.tail <= PAIR * TPB * P and self.tiles < DIGIT * DIGIT
        self.blocks = -(-(edges + WIDE) // BLOCK)
        assert self.blocks <= P
        self.early = min(3 * RING, (self.blocks - 1) // RING * RING)
        self.first_row = WIDE
        self.rows = WIDE + (self.blocks + 1) * BLOCK


class At:

    def __init__(self, b, slot, turn, ring):
        self.b, self.slot, self.turn, self.ring = b, slot, turn, ring

    def ahead(self, n):
        turns, slot = divmod(self.slot + n, self.ring)
        return At(self.b + n, slot, self.turn + turns, self.ring)

    def back(self, n):
        borrowed = (n - self.slot + self.ring - 1) // self.ring if n > self.slot else 0
        return At(self.b - n, self.slot - n + borrowed * self.ring, self.turn - borrowed, self.ring)

    def within(self, count, first=0):
        return not isinstance(self.b, int) or first <= self.b < count

    def at_least(self, n):
        return not isinstance(self.b, int) or self.b >= n


def each(engine, body, count, ring, drain=0, first=0):
    begin, turns = first // ring, (count - 1) // ring
    for b in range(first, min(first + ring, count)):
        body(At(b, b % ring, b // ring, ring))
    if turns > begin + 1:
        with engine.Fori(begin + 1, turns) as turn:
            for slot in range(ring):
                body(At(turn * ring + slot, slot, turn, ring))
    for b in range(ring * turns if turns > begin + 1 else min(first + ring, count), count + drain):
        body(At(b, b % ring, b // ring, ring))


@contextmanager
def phase_semaphores(nc, prefix=""):
    used = []
    with ExitStack() as ctx:
        def sem(name):
            used.append(ctx.enter_context(nc.semaphore(prefix + name)))
            return used[-1]

        yield sem
        with nc.Block() as block:
            @block.gpsimd
            def _(pool):
                for one in used[0::5]:
                    pool.sem_clear(one)

            @block.sync
            def _(sp):
                for one in used[1::5]:
                    sp.sem_clear(one)

            @block.scalar
            def _(act):
                for one in used[2::5]:
                    act.sem_clear(one)

            @block.vector
            def _(dve):
                for one in used[3::5]:
                    dve.sem_clear(one)

            @block.tensor
            def _(pe):
                for one in used[4::5]:
                    pe.sem_clear(one)


def setup_phase(nc, s, k, dram):
    NB = s.blocks
    full = s.edges // BLOCK
    rest = s.edges - full * BLOCK
    with ExitStack() as ctx:
        sb = lambda n, sh, dt=FP32: ctx.enter_context(nc.sbuf_tensor(n, sh, dt))
        sem = ctx.enter_context(phase_semaphores(nc))
        raw_i = [sb(f"raw_{n}", [NB, BLOCK], I32) for n in ("dst", "src", "type")]
        raw_f = [sb(f"rawf_{n}", [NB, BLOCK]) for n in ("dst", "src", "type", "weight")]
        next_i = sb("next_dst_i", [NB, BLOCK], I32)
        next_f = sb("next_dst", [NB, BLOCK])
        descents = sb("descents", [P, 1])
        raw_m = sb("raw_w0", [P, P])
        type_col = sb("type_col", [P, NB * CPB])
        w_col = sb("w_col", [P, NB * CPB])
        extremes = sb("extremes", [P, 2])
        ext_t = sb("ext_t", [2, 1])
        ext_d = sb("ext_d", [2, 2])
        ext_b = sb("ext_b", [P, 2])
        span = sb("span", [P, 2])
        ones = sb("ones_setup", [P, P])
        dst_int = sb("dst_int", [P, NB * CPB], I32)
        digit_i = [sb(f"digit_i{i}", [P, NB * CPB], I32) for i in range(2)]
        digit_f = [sb(f"digit_f{i}", [P, NB * CPB]) for i in range(2)]
        hot = [sb(f"digit_hot{i}", [P, NB * CPB, DIGIT], BF16) for i in range(2)]
        counts = sb("counts", [DIGIT, DIGIT])
        running = sb("running", [DIGIT, DIGIT])
        below = sb("below", [DIGIT, DIGIT])
        zeros_d = sb("zeros_digit", [DIGIT, DIGIT])
        starts = sb("starts", [DIGIT, DIGIT])
        row = sb("start_row", [1, DIGIT * DIGIT])
        size = sb("pair_size", [1, s.batches, PAIRS])
        crowd = sb("crowded", [1, s.batches])
        wide = sb("wide", [1, s.batches])
        calm = sb("calm", [1, s.batches])
        flag = sb("unsorted_flag", [1, 2])
        scratch = sb("table_scratch", [1, s.batches])
        scratch_i = sb("table_scratch_i", [1, s.batches], I32)
        need_i = sb("need_i", [1, s.batches], I32)
        need_f = sb("need_f", [1, s.batches])
        pads = sb("pad_rows", [P, CPB * ROW])
        bias_b = sb("bias_b", [P, P])
        bias_f = sb("bias_f", [3, P])
        part = [sb(f"part{j}", [3, P], BF16) for j in range(3)]
        left = [sb(f"left{j}", [3, P]) for j in range(2)]
        pick = [sb(f"pick{j}", [3, P]) for j in range(2)]
        tp = ctx.enter_context(nc.psum_tensor("tp_setup", [P, 4, CPB * P], FP32))
        small = ctx.enter_context(nc.psum_tensor("small_setup", [P, 4, CPB * P], FP32))
        loaded = sem("edges_loaded")
        padded = sem("padding_written")
        consts = sem("constants_made")
        dve_step = sem("setup_vector_step")
        floats_ready = sem("floats_ready")
        turned = sem("edges_transposed")
        columns_ready = sem("columns_ready")
        extremes_ready = sem("extremes_ready")
        extremes_turned = sem("extremes_transposed")
        diagonal_ready = sem("diagonal_ready")
        extremes_spread = sem("extremes_spread")
        hot_ready = sem("digits_ready")
        counted = sem("tiles_counted")
        running_ready = sem("running_ready")
        offsets_done = sem("offsets_done")
        starts_ready = sem("starts_ready")
        descents_ready = sem("descents_ready")
        descents_summed = sem("descents_summed")
        row_loaded = sem("start_row_loaded")
        pads_ready = sem("pads_ready")
        pads_stored = sem("pads_stored")

        loads = []
        arrays = (dram.dst, dram.src, dram.type, dram.w)
        blocks_of = lambda a, lo, n: a[lo:lo + BLOCK * n].rearrange("(b e) -> b e", e=BLOCK)
        line = lambda a, lo, hi: a[lo:hi].rearrange("(o e) -> o e", o=1)
        for n, (buf, arr) in enumerate(zip(raw_i + [raw_f[3]], arrays)):
            loads.append((buf[0:full, :], blocks_of(arr, 0, full)))
            if rest:
                loads.append((buf[full:full + 1, 0:rest], line(arr, full * BLOCK, s.edges)))
            if n:
                if rest:
                    loads.append((buf[full:full + 1, rest:BLOCK], line(arr, 0, BLOCK - rest)))
                done = full + (1 if rest else 0)
                if done < NB:
                    loads.append((buf[done:NB, :], blocks_of(arr, 0, NB - done)))
        after_full = (s.edges - 1) // BLOCK
        after_rest = s.edges - 1 - after_full * BLOCK
        loads.append((next_i[0:after_full, :], blocks_of(dram.dst, 1, after_full)))
        if after_rest:
            loads.append((next_i[after_full:after_full + 1, 0:after_rest],
                          line(dram.dst, 1 + after_full * BLOCK, s.edges)))
        for r, root in enumerate((dram.root1, dram.root2)):
            loads.append((k.root[r][:], root))
        for r, w in enumerate((dram.w1, dram.w2)):
            loads.append((k.wrel[r][:].rearrange("p (r n) -> p r n", r=RELATIONS), w.rearrange("r p n -> p r n")))
        loads.append((raw_m[:], dram.w0))
        for buf, b in ((bias_b, dram.b1), (bias_f, dram.b2)):
            loads.append((buf[:], b.rearrange("(o n) -> o n", o=1).to_broadcast(list(buf.shape))))

        block = ctx.enter_context(nc.Block())

        @block.sync
        def _(sp):
            sp.wait_ge(padded, 2)
            for out, in_ in loads:
                sp.dma_start(out, in_).then_inc(loaded, 16)
            sp.wait_ge(pads_ready, 1)
            sp.dma_start(dram.edge_rows[0:WIDE, :].rearrange("(p c) r -> p (c r)", c=WIDE // P),
                         pads[:, 0:WIDE // P * ROW]).then_inc(pads_stored, 16)
            last = s.first_row + s.blocks * BLOCK
            sp.dma_start(dram.edge_rows[last:last + BLOCK, :].rearrange("(p c) r -> p (c r)", c=CPB),
                         pads[:]).then_inc(pads_stored, 16)
            sp.wait_ge(starts_ready, 1)
            sp.dma_start(dram.starts.rearrange("o (a b) -> (o a) b", b=DIGIT), starts[:]).then_inc(row_loaded, 16)
            sp.wait_ge(row_loaded, 16)
            sp.dma_start(row[:], dram.starts).then_inc(row_loaded, 16)
            sp.wait_ge(row_loaded, 32)
            sp.wait_ge(pads_stored, 32)

        @block.gpsimd
        def _(pool):
            nc.gpsimd.memset(ones[:], 1.0).then_inc(consts, 1)
            nc.gpsimd.iota(k.node[:], pattern=[[1, TPB * P]], base=0, channel_multiplier=0,
                           allow_small_or_imprecise_dtypes=True).then_inc(consts, 1)
            nc.gpsimd.iota(k.minus_base[:], pattern=[[-TPB * P, s.batches]], base=0, channel_multiplier=0,
                           allow_small_or_imprecise_dtypes=True).then_inc(consts, 1)
            pool.wait_ge(consts, 3)
            nc.gpsimd.affine_select(out=k.ident[:], in_=ones[:], compare_op=ALU.is_equal, fill=0.0,
                                    base=0, pattern=[[-1, P]], channel_multiplier=1).then_inc(consts, 1)
            nc.gpsimd.affine_select(out=below[:], in_=ones[0:DIGIT, 0:DIGIT], compare_op=ALU.is_gt, fill=0.0,
                                    base=0, pattern=[[1, DIGIT]], channel_multiplier=-1).then_inc(consts, 1)
            nc.gpsimd.memset(k.gather_ring[:], 0.0).then_inc(k.marked, 1)
            pool.wait_ge(k.marked, 1)
            if s.early:
                pool.wait_ge(columns_ready, 1)
                gather_and_store(nc, pool, s, k, dram, 0, s.early)

        @block.vector
        def _(dve):
            v = nc.vector
            made = [0]

            def link(ins, ready=None):
                made[0] += 1
                ins.then_inc(dve_step, 1)
                dve.wait_ge(dve_step, made[0])
                if ready is not None:
                    dve.sem_inc(ready, 1)

            v.memset(raw_i[0][:], int(NO_NODE)).then_inc(padded, 1)
            v.memset(next_i[:], int(NO_NODE)).then_inc(padded, 1)
            link(v.memset(k.zeros[:], 0.0))
            link(v.memset(k.ones3[:], 1.0))
            link(v.memset(zeros_d[:], 0.0))
            link(v.memset(pads[:], 0.0))
            pad_dst = pads[:].rearrange("p (c r) -> p c r", r=ROW)[:, :, P:P + 1]
            link(v.memset(pad_dst, NO_NODE), pads_ready)
            dve.wait_ge(consts, 5)
            dve.wait_ge(loaded, 16 * len(loads))
            for n in range(3):
                link(v.tensor_copy(raw_f[n][:], raw_i[n][:]), floats_ready if n == 2 else None)
            link(v.tensor_copy(next_f[:], next_i[:]))
            link(v.tensor_tensor(next_f[:], next_f[:], raw_f[0][:], ALU.is_lt))
            link(v.memset(descents[:], 0.0))
            link(v.tensor_reduce(descents[0:NB, :], next_f[:], AX.X, ALU.add), descents_ready)
            col = lambda t: t[:].rearrange("p (b c) -> p c b", c=CPB)
            dve.wait_ge(turned, 1)
            for n, out in enumerate((k.dst_col, k.src_col, type_col, w_col)):
                link(v.tensor_copy(col(out), tp[:, n].rearrange("p (c b) -> p c b", c=CPB)[:, :, 0:NB]),
                     columns_ready if out is k.src_col else None)
            link(v.tensor_reduce(extremes[:, 0:1], w_col[:], AX.X, ALU.max))
            link(v.tensor_reduce(extremes[:, 1:2], w_col[:], AX.X, ALU.min))
            link(v.tensor_scalar(extremes[:, 1:2], extremes[:, 1:2], -1.0, None, ALU.mult), extremes_ready)
            dve.wait_ge(extremes_turned, 1)
            link(v.tensor_reduce(ext_t[:], small[0:2, 0, 0:P], AX.X, ALU.max))
            link(v.tensor_scalar(ext_d[:], k.ident[0:2, 0:2], ext_t[:, 0:1], None, ALU.mult), diagonal_ready)
            link(v.tensor_copy(k.w0t[:], small[:, 1, 0:P]))
            dve.wait_ge(extremes_spread, 1)
            link(v.tensor_copy(ext_b[:], small[:, 2, 0:2]))
            link(v.tensor_scalar(span[:, 0:1], ext_b[:, 0:1], ext_b[:, 1:2], EW_EPS, ALU.add, ALU.add))
            link(v.reciprocal(span[:, 1:2], span[:, 0:1]))
            link(v.tensor_scalar(w_col[:], w_col[:], ext_b[:, 1:2], span[:, 1:2], ALU.add, ALU.mult))
            coef = k.coef[:].rearrange("p (q r) -> p q r", r=RELATIONS)
            for r in range(RELATIONS):
                link(v.scalar_tensor_tensor(out=coef[:, :, r], in0=type_col[:], scalar=float(r), in1=w_col[:],
                                            op0=ALU.is_equal, op1=ALU.mult))
            link(v.tensor_copy(dst_int[:], k.dst_col[:]))
            link(v.tensor_scalar(digit_i[0][:], dst_int[:], 12, None, ALU.arith_shift_right))
            link(v.tensor_scalar(digit_i[1][:], dst_int[:], 7, DIGIT - 1, ALU.arith_shift_right, ALU.bitwise_and))
            for i in range(2):
                link(v.tensor_copy(digit_f[i][:], digit_i[i][:]))
            for i in range(2):
                for d in range(DIGIT):
                    ins = v.tensor_scalar(hot[i][:, :, d], digit_f[i][:], float(d), None, ALU.is_equal)
                    if d < DIGIT - 1:
                        made[0] += 1
                        ins.then_inc(dve_step, 1)
                link(ins, hot_ready)
            dve.wait_ge(counted, 1)
            link(v.tensor_copy(counts[:], small[0:DIGIT, 3, 0:DIGIT]))
            link(v.tensor_tensor_scan(running[:], zeros_d[:], counts[:], 0.0, ALU.add, ALU.add), running_ready)
            dve.wait_ge(offsets_done, 1)
            link(v.tensor_tensor(starts[:], running[:], counts[:], ALU.subtract))
            link(v.tensor_scalar(starts[:], starts[:], small[0:DIGIT, 3, 64:65], None, ALU.add), starts_ready)
            dve.wait_ge(descents_summed, 1)
            link(v.tensor_scalar(flag[:, 0:1], small[0:1, 0, 200:201], 0.5, None, ALU.is_gt))
            link(v.tensor_scalar(flag[:, 1:2], flag[:, 0:1], -1.0, 1.0, ALU.mult, ALU.add))
            dve.wait_ge(row_loaded, 32)
            B = s.batches
            per = TPB // PAIRS
            every = lambda first, n: row[:, first:first + s.tiles].rearrange("o (b j) -> o b j", j=n)
            pair_start = every(0, per)[:, :, 0].rearrange("o (b i) -> o b i", i=PAIRS)
            pair_end = every(per, per)[:, :, 0].rearrange("o (b i) -> o b i", i=PAIRS)
            batch_start = every(0, TPB)[:, :, 0]
            batch_end = every(TPB, TPB)[:, :, 0]
            link(v.tensor_tensor(size[:], pair_end, pair_start, ALU.subtract))
            link(v.tensor_reduce(crowd[:], size[:], AX.X, ALU.max))
            link(v.tensor_scalar(wide[:], crowd[:], float(P), flag[:, 0:1], ALU.is_gt, ALU.max))
            link(v.tensor_scalar(crowd[:], crowd[:], float(WIDE), flag[:, 0:1], ALU.is_gt, ALU.max))
            link(v.tensor_scalar(calm[:], crowd[:], -1.0, 1.0, ALU.mult, ALU.add))
            link(v.tensor_tensor(scratch[:], batch_end, batch_start, ALU.subtract))
            link(v.tensor_scalar(scratch[:], scratch[:], float(BLOCK - 1), None, ALU.add))
            link(v.tensor_copy(scratch_i[:], scratch[:]))
            link(v.tensor_scalar(scratch_i[:], scratch_i[:], 9, None, ALU.arith_shift_right))
            link(v.tensor_copy(scratch[:], scratch_i[:]))
            link(v.tensor_tensor(scratch[:], scratch[:], crowd[:], ALU.mult))
            link(v.tensor_scalar(scratch[:], scratch[:], flag[:, 1:2], None, ALU.mult))
            link(v.tensor_scalar(need_f[:], crowd[:], flag[:, 0:1], float(NB), ALU.mult, ALU.mult))
            link(v.tensor_tensor(scratch[:], scratch[:], need_f[:], ALU.add))
            link(v.tensor_tensor(scratch[:], scratch[:], wide[:], ALU.add))
            link(v.memset(k.kind[:], 0))
            link(v.tensor_copy(k.kind[:, 0:s.batches], scratch[:]))
            table = k.table[:].rearrange("o (b j) -> o b j", j=4)
            link(v.tensor_scalar(scratch[:], batch_start, flag[:, 1:2], float(s.first_row), ALU.mult, ALU.add))
            link(v.tensor_copy(table[:, :, 0], scratch[:]))
            link(v.tensor_copy(need_i[:], batch_end))
            link(v.tensor_scalar(need_i[:], need_i[:], 9, None, ALU.arith_shift_right))
            link(v.tensor_copy(scratch[:], need_i[:]))
            link(v.tensor_scalar(need_f[:], crowd[:], flag[:, 0:1], float(NB), ALU.mult, ALU.mult))
            link(v.tensor_scalar(scratch[:], scratch[:], 2.0, float(NB), ALU.add, ALU.min))
            link(v.tensor_tensor(scratch[:], scratch[:], need_f[:], ALU.max))
            link(v.tensor_copy(table[:, :, 1], scratch[:]))
            for i in range(PAIRS):
                link(v.tensor_scalar(scratch[:], pair_start[:, :, i], float(s.first_row), None, ALU.add))
                link(v.tensor_tensor(scratch[:], scratch[:], calm[:], ALU.mult))
                link(v.tensor_copy(table[:, :, 2 + i], scratch[:]))
            for j in range(TPB):
                link(v.tensor_copy(k.bias_rows[:, j], bias_b[:]))
            link(v.tensor_copy(part[0][:], bias_f[:]))
            link(v.tensor_tensor(left[0][:], bias_f[:], part[0][:], ALU.subtract))
            link(v.tensor_copy(part[1][:], left[0][:]))
            link(v.tensor_tensor(left[1][:], left[0][:], part[1][:], ALU.subtract))
            link(v.tensor_copy(part[2][:], left[1][:]))
            link(v.tensor_scalar(pick[0][:], part[0][:], k.ident[0:3, 0:1], None, ALU.mult))
            for j in (1, 2):
                link(v.scalar_tensor_tensor(out=pick[j % 2][:], in0=part[j][:], scalar=k.ident[0:3, j:j + 1],
                                            in1=pick[(j + 1) % 2][:], op0=ALU.mult, op1=ALU.add))
            for j in range(TPB):
                link(v.tensor_copy(k.bias_parts[:, P * j:P * (j + 1)], pick[0][:]))

        @block.tensor
        def _(pe):
            pe.wait_ge(consts, 5)
            pe.wait_ge(floats_ready, 1)
            for n in range(4):
                edges = raw_f[n][:].rearrange("b (p c) -> b c p", c=CPB)
                for c in range(CPB):
                    last = nc.tensor.transpose(tp[:, n, P * c:P * c + NB], edges[:, c, :], k.ident[0:NB, 0:NB])
            last.then_inc(turned, 1)
            pe.wait_ge(extremes_ready, 1)
            nc.tensor.transpose(small[0:2, 0, 0:P], extremes[:], k.ident[:])
            nc.tensor.transpose(small[:, 1, 0:P], raw_m[:], k.ident[:]).then_inc(extremes_turned, 1)
            pe.wait_ge(diagonal_ready, 1)
            nc.tensor.matmul(small[:, 2, 0:2], ones[0:2, :], ext_d[:], start=True, stop=True).then_inc(extremes_spread, 1)
            pe.wait_ge(hot_ready, 2)
            for q in range(NB * CPB):
                last = nc.tensor.matmul(small[0:DIGIT, 3, 0:DIGIT], hot[0][:, q, :], hot[1][:, q, :],
                                        start=(q == 0), stop=(q == NB * CPB - 1))
            last.then_inc(counted, 1)
            pe.wait_ge(running_ready, 1)
            nc.tensor.matmul(small[0:DIGIT, 3, 64:65], below[:], running[:, DIGIT - 1:DIGIT], start=True,
                             stop=True).then_inc(offsets_done, 1)
            pe.wait_ge(descents_ready, 1)
            nc.tensor.matmul(small[0:1, 0, 200:201], ones[:, 0:1], descents[:], start=True,
                             stop=True).then_inc(descents_summed, 1)


class Sums:

    def __init__(self, nc, ctx, sem, s, k, dram, name, transposed):
        self.nc, self.s, self.k, self.rows, self.transposed = nc, s, k, dram.edge_rows, transposed
        sb = lambda n, sh: ctx.enter_context(nc.sbuf_tensor(f"{name}_{n}", sh, FP32))
        self.window = sb("window", [P, UNROLL, PAIRS, WIDE // P, ROW])
        self.ends = sb("ends", [P, 2, TPB, P])
        self.second_ends = sb("second_ends", [P, TPB, P])
        self.step = sb("step", [P, CPB, ROW])
        self.step_ends = sb("step_ends", [P, CPB, TPB, P])
        self.loaded = [sem(f"windows_loaded{i}") for i in range(UNROLL)]
        self.built = sem("ends_built")
        self.added = sem("windows_added")
        self.second_free = sem("second_free")
        self.second_built = sem("second_built")
        self.chunk_free = [sem(f"chunk_free{i}") for i in range(CPB)]
        self.chunk_loaded = [sem(f"chunk_loaded{i}") for i in range(CPB)]
        self.chunk_built = [sem(f"chunk_built{i}") for i in range(CPB)]
        self.kinds = {}

    def kind_of(self, engine, at):
        if at.slot % KINDS == 0:
            _, self.kinds[engine.engine] = self.nc.values_load_multi_w_load_instructions(
                self.k.kind[0:1, bass.ds(at.b, KINDS)], engines=[engine.engine], min_val=0, max_val=self.s.blocks + 1,
                skip_runtime_bounds_check_because="worked out on the chip from counts of the edges")
        return self.kinds[engine.engine][at.slot % KINDS]

    def load(self, sp, at, stored):
        _, (first, need, *starts) = self.nc.values_load_multi_w_load_instructions(
            self.k.table[0:1, bass.ds(at.b * 4, 4)], engines=[sp.engine], min_val=0, max_val=self.s.rows - BLOCK,
            skip_runtime_bounds_check_because="counts of edges behind the first padding, which a block of padding follows")
        kind = self.kind_of(sp, at)
        if stored is not None:
            sp.wait_ge(stored, self.nc.s_assert_within(need, 1, self.s.blocks))
            sp.sem_inc(self.k.passed, 1)
        if at.at_least(UNROLL):
            sp.wait_ge(self.added, at.b - UNROLL + 1)
        sp.sem_inc(self.k.passed, 1)
        with sp.If(kind > 0):
            for i in range(PAIRS):
                sp.dma_start(self.window[:, at.slot, i],
                             self.rows[bass.ds(starts[i], WIDE), :].rearrange("(c p) r -> p c r", p=P)
                             ).then_inc(self.loaded[at.slot], 16)
            with sp.If(kind > 1):
                with sp.Fori(1, kind) as x:
                    for c in range(CPB):
                        row = self.nc.s_assert_within(
                            first + (x - 1) * BLOCK + c * P, 0, self.s.rows - P,
                            skip_runtime_bounds_check_because="a block of padding follows the batch's rows")
                        sp.wait_ge(self.chunk_free[c], 1)
                        sp.sem_clear(self.chunk_free[c])
                        sp.dma_start(self.step[:, c], self.rows[bass.ds(row, P), :]).then_inc(self.chunk_loaded[c], 16)
        with sp.Else():
            for i in range(PAIRS):
                sp.dma_start(self.window[:, at.slot, i, 0], self.rows[bass.ds(starts[i], P), :]
                             ).then_inc(self.loaded[at.slot], 16)

    def begin(self, dve):
        dve.sem_inc(self.second_free, 1)
        for c in range(CPB):
            dve.sem_inc(self.chunk_free[c], 1)

    def match(self, at, ends, destinations, tiles):
        split = lambda t: t[:, tiles.start * P:tiles.stop * P]
        return self.nc.vector.tensor_scalar(split(ends.rearrange("p t n -> p (t n)")), split(self.k.node[:]),
                                            destinations, self.k.minus_base[:, bass.ds(at.b, 1)], ALU.subtract,
                                            ALU.is_equal)

    def build_steps(self, dve, at):
        kind = self.kind_of(dve, at)
        with dve.If(kind > 0):
            with dve.If(kind > 1):
                with dve.Fori(1, kind) as x:
                    for c in range(CPB):
                        dve.wait_ge(self.chunk_loaded[c], 16)
                        dve.sem_clear(self.chunk_loaded[c])
                        self.match(at, self.step_ends[:, c], self.step[:, c, P:P + 1],
                                   range(TPB)).then_inc(self.chunk_built[c], 1)
            dve.wait_ge(self.loaded[at.slot], (at.turn + 1) * 16 * PAIRS)
            dve.sem_inc(self.k.passed, 1)
            dve.wait_ge(self.second_free, 1)
            dve.sem_clear(self.second_free)
            for i in range(PAIRS):
                last = self.match(at, self.second_ends[:], self.window[:, at.slot, i, 1, P:P + 1], TILES_OF_PAIR[i])
            last.then_inc(self.second_built, 1)

    def build(self, dve, at):
        dve.wait_ge(self.loaded[at.slot], (at.turn + 1) * 16 * PAIRS)
        if at.at_least(2):
            dve.wait_ge(self.added, at.b - 1)
        for i in range(PAIRS):
            last = self.match(at, self.ends[:, at.slot % 2], self.window[:, at.slot, i, 0, P:P + 1], TILES_OF_PAIR[i])
        last.then_inc(self.built, 1)

    def products(self, bank, ends, rows, tiles):
        if self.transposed:
            return self.nc.tensor.matmul(bank[:, tiles.start:tiles.stop].rearrange("p t n -> p (t n)"), rows,
                                         ends[:, tiles.start:tiles.stop].rearrange("p t n -> p (t n)"), start=False,
                                         stop=True, skip_group_check=True)
        for j in tiles:
            last = self.nc.tensor.matmul(bank[:, j], ends[:, j], rows, start=False, stop=True, skip_group_check=True)
        return last

    def add_steps(self, pe, at, bank):
        kind = self.kind_of(pe, at)
        with pe.If(kind > 0):
            with pe.If(kind > 1):
                with pe.Fori(1, kind) as x:
                    for c in range(CPB):
                        pe.wait_ge(self.chunk_built[c], 1)
                        pe.sem_clear(self.chunk_built[c])
                        self.products(bank, self.step_ends[:, c], self.step[:, c, 0:P],
                                      range(TPB)).then_inc(self.chunk_free[c], 1)
            pe.wait_ge(self.second_built, 1)
            pe.sem_clear(self.second_built)
            for i in range(PAIRS):
                last = self.products(bank, self.second_ends, self.window[:, at.slot, i, 1, 0:P], TILES_OF_PAIR[i])
            last.then_inc(self.second_free, 1)

    def add_windows(self, pe, at, bank):
        pe.wait_ge(self.built, at.b + 1)
        for i in range(PAIRS):
            last = self.products(bank, self.ends[:, at.slot % 2], self.window[:, at.slot, i, 0, 0:P], TILES_OF_PAIR[i])
        last.then_inc(self.added, 1)


def gathered_blocks(s, phase, slot, turns):
    return (turns + phase * len(range(slot, s.blocks, RING))) * (16 * CPB)


def stage_index(nc, k, at, index, staged):
    nc.gpsimd.tensor_copy(index[:, at.slot, :], k.src_col[:, bass.ds(at.b * CPB, CPB)]).then_inc(staged, 1)


def gather_block(nc, pool, k, table, ring, at, index, staged, gathered):
    pool.wait_ge(staged, at.b + 1)
    pool.sem_inc(k.passed, 1)
    for c in range(CPB):
        nc.gpsimd.indirect_dma_start(
            out=ring[:, at.slot, c, 0:P], out_offset=None, in_=table,
            in_offset=bass.IndirectOffsetOnAxis(ap=index[:, at.slot, c:c + 1], axis=0)).then_inc(gathered[at.slot], 16)


def gather_and_store(nc, pool, s, k, dram, first, last):
    landed = lambda at, turns: gathered_blocks(s, 0, at.slot, turns)

    def body(at):
        store, told, after = at.back(1), at.back(3), at.ahead(1)
        if store.within(last, first):
            pool.wait_ge(k.marked, store.b + 2)
            pool.sem_inc(k.passed, 1)
            pool.wait_ge(k.gathered[store.slot], landed(store, store.turn + 1))
            pool.dma_start(block_rows(dram, s, store), k.gather_ring[:, store.slot].rearrange("p c r -> p (c r)")
                           ).then_inc(k.rows_stored[store.slot], 16)
        if told.within(last, first):
            pool.wait_ge(k.rows_stored[told.slot], (told.turn + 1) * 16)
            pool.sem_inc(k.blocks_stored, 1)
        if after.within(last, first):
            if after.at_least(RING):
                pool.wait_ge(k.gathered[after.slot], landed(after, after.turn))
            stage_index(nc, k, after, k.index, k.staged)
        if at.within(last, first):
            if at.at_least(RING):
                pool.wait_ge(k.rows_stored[at.slot], at.turn * 16)
            nc.gpsimd.tensor_copy(k.gather_ring[:, at.slot, :, P],
                                  k.dst_col[:, bass.ds(at.b * CPB, CPB)]).then_inc(k.marked, 1)
            gather_block(nc, pool, k, dram.x, k.gather_ring, at, k.index, k.staged, k.gathered)

    stage_index(nc, k, At(first, first % RING, first // RING, RING), k.index, k.staged)
    each(pool, body, last, RING, drain=3, first=first)


def block_rows(dram, s, at):
    return dram.edge_rows[bass.ds(at.b * BLOCK + s.first_row, BLOCK), :].rearrange("(p c) r -> p (c r)", c=CPB)


class Norm:

    SLOTS = 4

    def __init__(self, nc, ctx, sem, name):
        self.nc = nc
        sb = lambda n, sh: ctx.enter_context(nc.sbuf_tensor(f"{name}_{n}", sh, FP32))
        self.v = sb("to_norm", [P, self.SLOTS, TPB, P])
        self.stats = sb("bn_stats", [P, self.SLOTS, TPB, nc.vector.BN_STATS_DIM])
        self.moments = sb("moments", [P, self.SLOTS, TPB, nc.vector.BN_AGGR_DIM])
        self.std = sb("std", [P, self.SLOTS, TPB])
        self.rstd = sb("rstd", [P, self.SLOTS, TPB])
        self.shift = sb("shift", [P, self.SLOTS, TPB])
        self.eps = sb("eps", [P, 1])
        self.out = sb("normed", [P, UNROLL, TPB, P])
        self.summed = sem("summed")
        self.stats_done = sem("stats_done")
        self.moments_begun = sem("moments_begun")
        self.moments_done = sem("moments_done")
        self.std_done = sem("std_done")
        self.rstd_done = sem("rstd_done")
        self.shift_done = sem("shift_done")
        self.normed = sem("normed")
        self.eps_made = sem("eps_made")

    def constants(self):
        self.nc.vector.memset(self.eps[:], LN_EPS).then_inc(self.eps_made, 1)

    def sum(self, dve, at, update, rows):
        if at.at_least(self.SLOTS):
            dve.wait_ge(self.normed, (at.b - self.SLOTS + 1) * TPB)
        self.nc.vector.tensor_tensor(self.v[:, at.slot % self.SLOTS], update, rows, ALU.add).then_inc(self.summed, 1)

    def statistics(self, dve, at):
        h = at.slot % self.SLOTS
        dve.wait_ge(self.summed, at.b + 1)
        for j in range(TPB):
            last = self.nc.vector.bn_stats(self.stats[:, h, j, :], self.v[:, h, j, :])
        last.then_inc(self.stats_done, 1)

    def aggregate(self, dve, at):
        h = at.slot % self.SLOTS
        dve.wait_ge(self.stats_done, at.b + 1)
        dve.sem_inc(self.moments_begun, 1)
        for j in range(TPB):
            last = self.nc.vector.bn_aggr(self.moments[:, h, j, :], self.stats[:, h, j, :])
        last.then_inc(self.moments_done, 1)

    def deviation(self, act, at):
        h = at.slot % self.SLOTS
        act.wait_ge(self.moments_done, at.b + 1)
        self.nc.scalar.activation(self.std[:, h, :], self.moments[:, h, :, 1], ACT.Sqrt,
                                  bias=self.eps[:]).then_inc(self.std_done, 1)

    def invert(self, dve, at):
        h = at.slot % self.SLOTS
        dve.wait_ge(self.std_done, at.b + 1)
        self.nc.vector.reciprocal(self.rstd[:, h, :], self.std[:, h, :]).then_inc(self.rstd_done, 1)

    def offset(self, dve, at):
        h = at.slot % self.SLOTS
        dve.wait_ge(self.rstd_done, at.b + 1)
        self.nc.vector.scalar_tensor_tensor(out=self.shift[:, h, :], in0=self.moments[:, h, :, 0], scalar=-1.0,
                                            in1=self.rstd[:, h, :], op0=ALU.mult,
                                            op1=ALU.mult).then_inc(self.shift_done, 1)

    def apply(self, act, at, stored):
        h = at.slot % self.SLOTS
        act.wait_ge(self.shift_done, at.b + 1)
        if at.at_least(UNROLL):
            act.wait_ge(stored[at.slot // PAIR], at.turn * 16)
        for j in range(TPB):
            self.nc.scalar.activation(self.out[:, at.slot, j, :], self.v[:, h, j, :], ACT.Identity,
                                      bias=self.shift[:, h, j:j + 1],
                                      scale=self.rstd[:, h, j:j + 1]).then_inc(self.normed, 1)


def pair_rows(array, at):
    return array[bass.ds(at.b * (TPB * P), PAIR * TPB * P), :].rearrange("(t p) f -> p t f", p=P)


def pair_slots(ring, at):
    return ring[:, at.slot:at.slot + PAIR].rearrange("p b t f -> p (b t) f")


def is_last(s, at):
    return isinstance(at.b, int) and at.b == s.batches - PAIR and s.tail < PAIR * TPB * P


def load_pair(sp, s, k, array, at, ring, loaded, zeroed, padded=True):
    out = pair_slots(ring, at)
    if padded or not is_last(s, at):
        sp.dma_start(out, pair_rows(array, at)).then_inc(loaded[at.slot // PAIR], 16)
        return
    whole, rest = divmod(s.tail, P)
    base = at.b * TPB * P
    tiles = PAIR * TPB
    for first in range(whole, tiles, TPB):
        n = min(TPB, tiles - first)
        sp.dma_start(out[:, first:first + n], k.zeros[:, 0:n * P].rearrange("p (t f) -> p t f", f=P)
                     ).then_inc(zeroed, 16)
    done = 16 * len(range(whole, tiles, TPB))
    sp.wait_ge(zeroed, done)
    parts = []
    if whole:
        parts.append((out[:, 0:whole], array[base:base + whole * P, :].rearrange("(t p) f -> p t f", p=P)))
    if rest:
        parts.append((out[0:rest, whole], array[base + whole * P:s.nodes, :]))
    for o, i in parts[:-1]:
        sp.dma_start(o, i).then_inc(zeroed, 16)
        sp.wait_ge(zeroed, done + 16)
    sp.dma_start(*parts[-1]).then_inc(loaded[at.slot // PAIR], 16)


def store_pair(sp, s, array, at, ring, stored, padded):
    src = pair_slots(ring, at)
    if padded or not is_last(s, at):
        sp.dma_start(pair_rows(array, at), src).then_inc(stored[at.slot // PAIR], 16)
        return
    whole, rest = divmod(s.tail, P)
    base = at.b * TPB * P
    if whole:
        sp.dma_start(array[base:base + whole * P, :].rearrange("(t p) f -> p t f", p=P),
                     src[:, 0:whole]).then_inc(stored[at.slot // PAIR], 16)
    if rest:
        sp.dma_start(array[base + whole * P:s.nodes, :], src[0:rest, whole]).then_inc(stored[at.slot // PAIR], 16)


def wait_stored(sp, s, stored, padded):
    pieces = 1 if padded or s.tail == PAIR * TPB * P else (s.tail >= P) + (s.tail % P > 0)
    pairs = s.batches // PAIR
    for slot in range(UNROLL // PAIR):
        n = len(range(slot, pairs, UNROLL // PAIR))
        last = slot == (pairs - 1) % (UNROLL // PAIR)
        sp.wait_ge(stored[slot], 16 * (n + (pieces - 1 if last else 0)))


def first_phase(nc, s, k, dram):
    with ExitStack() as ctx:
        sem = ctx.enter_context(phase_semaphores(nc, "l0_"))
        sums = Sums(nc, ctx, sem, s, k, dram, "l0", True)
        norm = Norm(nc, ctx, sem, "l0")
        sb = lambda n, sh, dt=FP32: ctx.enter_context(nc.sbuf_tensor(n, sh, dt))
        ps = lambda n: ctx.enter_context(nc.psum_tensor(n, [P, TPB, P], FP32))
        x_ring = sb("x_ring", [P, UNROLL, TPB, P])
        zt = sb("zt", [P, 2, TPB, P])
        zt_ps = [ps(f"zt_ps{i}") for i in range(2)]
        update_ps = [ps(f"update{i}") for i in range(2)]
        x_loaded = [sem(f"x_loaded{i}") for i in range(UNROLL // PAIR)]
        x_zeroed = sem("x_zeroed")
        stored = [sem(f"x1_stored{i}") for i in range(UNROLL // PAIR)]
        zt_done = sem("zt_copied")
        update_done = sem("update_done")
        B = s.batches
        block = ctx.enter_context(nc.Block())

        @block.sync
        def _(sp):
            def body(at):
                if at.within(B):
                    if at.slot % PAIR == 0:
                        if at.at_least(UNROLL):
                            sp.wait_ge(norm.summed, at.b - UNROLL + PAIR)
                            sp.sem_inc(k.passed, 1)
                        load_pair(sp, s, k, dram.x, at, x_ring, x_loaded, x_zeroed, False)
                    sums.load(sp, at, k.blocks_stored)

            each(sp, body, B, UNROLL)

        @block.gpsimd
        def _(pool):
            gather_and_store(nc, pool, s, k, dram, s.early, s.blocks)

        @block.vector
        def _(dve):
            norm.constants()
            sums.begin(dve)

            def body(at):
                two, three, four = at.back(2), at.back(3), at.back(4)
                if at.within(B):
                    sums.build_steps(dve, at)
                    sums.build(dve, at)
                if three.within(B):
                    norm.aggregate(dve, three)
                if four.within(B):
                    norm.invert(dve, four)
                if two.within(B):
                    dve.wait_ge(update_done, two.b + 1)
                    norm.sum(dve, two, update_ps[two.slot % 2][:], x_ring[:, two.slot])
                if four.within(B):
                    norm.offset(dve, four)
                if two.within(B):
                    norm.statistics(dve, two)

            each(dve, body, B, UNROLL, drain=4)

        @block.tensor
        def _(pe):
            def body(at):
                if at.within(B):
                    bank = zt_ps[at.slot % 2]
                    pe.wait_ge(x_loaded[at.slot // PAIR], (at.turn + 1) * 16)
                    if at.at_least(2):
                        pe.wait_ge(zt_done, at.b - 1)
                    for j in range(TPB):
                        nc.tensor.matmul(bank[:, j], x_ring[:, at.slot, j], k.ident[:], start=(j == 0), stop=True,
                                         skip_group_check=True)
                    sums.add_steps(pe, at, bank)
                    sums.add_windows(pe, at, bank)
                prev = at.back(1)
                if prev.within(B):
                    pe.wait_ge(zt_done, prev.b + 1)
                    if prev.at_least(2):
                        pe.wait_ge(norm.summed, prev.b - 1)
                    for j in range(TPB):
                        last = nc.tensor.matmul(update_ps[prev.slot % 2][:, j], zt[:, prev.slot % 2, j], k.w0t[:],
                                                start=True, stop=True)
                    last.then_inc(update_done, 1)

            each(pe, body, B, UNROLL, drain=1)

        @block.scalar
        def _(act):
            act.wait_ge(norm.eps_made, 1)

            def body(at):
                prev, three, four, out = at.back(1), at.back(3), at.back(4), at.back(6)
                if prev.within(B):
                    act.wait_ge(sums.added, prev.b + 1)
                    if prev.at_least(2):
                        act.wait_ge(update_done, prev.b - 1)
                    nc.scalar.copy(zt[:, prev.slot % 2], zt_ps[prev.slot % 2][:]).then_inc(zt_done, 1)
                if three.within(B):
                    norm.deviation(act, three)
                if four.within(B):
                    norm.apply(act, four, stored)
                if out.within(B) and out.slot % PAIR == 0:
                    act.wait_ge(norm.normed, (out.b + PAIR) * TPB)
                    act.sem_inc(k.passed, 1)
                    store_pair(act, s, dram.x1, out, norm.out, stored, True)

            each(act, body, B, UNROLL, drain=5)
            wait_stored(act, s, stored, True)


def message_phase(nc, s, k, dram, layer, table):
    name = f"m{layer}"
    with ExitStack() as ctx:
        sem = ctx.enter_context(phase_semaphores(nc, f"{name}_"))
        sb = lambda n, sh, dt=FP32: ctx.enter_context(nc.sbuf_tensor(f"{name}_{n}", sh, dt))
        ring = sb("rows_ring", [P, RING, CPB, P])
        index = sb("index", [P, RING, CPB], I32)
        rows_t = sb("rows_t", [P, 2, P])
        partial = sb("partial", [P, CPB, 3, P])
        messages = sb("messages", [P, RING, CPB, ROW])
        turned_ps = ctx.enter_context(nc.psum_tensor(f"{name}_turned_ps", [P, 2, 4 * P], FP32))
        product_ps = ctx.enter_context(nc.psum_tensor(f"{name}_product_ps", [P, CPB, 4 * P], FP32))
        gathered = k.gathered
        landed = lambda at, turns: gathered_blocks(s, 1 + layer, at.slot, turns)
        stored = [sem(f"stored{i}") for i in range(RING)]
        staged = sem("index_staged")
        turned = sem("turned")
        rows_t_done = sem("rows_t_copied")
        product_done = sem("product_done")
        part0_done = sem("part0_done")
        added = sem("parts_added")
        message_done = sem("message_done")
        cleared = sem("cleared")
        marked = sem("marked")
        wrel = k.wrel[layer]
        B = s.blocks
        coef = lambda c, r: k.coef[:, bass.ds(c * RELATIONS + r, 1)]
        block = ctx.enter_context(nc.Block())

        @block.gpsimd
        def _(pool):
            def body(at):
                after = at.ahead(1)
                if after.within(B):
                    if after.at_least(RING):
                        pool.wait_ge(gathered[after.slot], landed(after, after.turn))
                    stage_index(nc, k, after, index, staged)
                if at.at_least(RING):
                    pool.wait_ge(turned, (at.b - RING + 1) * CPB)
                    pool.sem_inc(k.passed, 1)
                gather_block(nc, pool, k, table, ring, at, index, staged, gathered)

            stage_index(nc, k, At(0, 0, 0, RING), index, staged)
            each(pool, body, B, RING)

        @block.tensor
        def _(pe):
            def turn(at, i):
                c = at.b * CPB + i
                if i == 0:
                    pe.wait_ge(gathered[at.slot], landed(at, at.turn + 1))
                if at.at_least(1) or i >= 2:
                    pe.wait_ge(rows_t_done, c - 1)
                nc.tensor.transpose(turned_ps[:, i % 2, 0:P], ring[:, at.slot, i],
                                    k.ident[:]).then_inc(turned, 1)

            def body(at):
                for i in range(CPB):
                    c = at.b * CPB + i
                    if i < CPB - 1:
                        turn(at, i + 1)
                    elif at.ahead(1).within(B):
                        turn(at.ahead(1), 0)
                    pe.wait_ge(rows_t_done, c + 1)
                    if at.at_least(1):
                        pe.wait_ge(message_done, c - CPB + 1)
                    nc.tensor.matmul(product_ps[:, i], rows_t[:, i % 2], wrel[:], start=True,
                                     stop=True).then_inc(product_done, 1)

            turn(At(0, 0, 0, RING), 0)
            each(pe, body, B, RING)

        @block.scalar
        def _(act):
            def copy_rows(c, i):
                act.wait_ge(turned, c + 1)
                if not isinstance(c, int) or c >= 2:
                    act.wait_ge(product_done, c - 1)
                nc.scalar.copy(rows_t[:, i % 2], turned_ps[:, i % 2, 0:P]).then_inc(rows_t_done, 1)

            def body(at):
                for i in range(CPB):
                    c = at.b * CPB + i
                    last = isinstance(at.b, int) and at.b == B - 1 and i == CPB - 1
                    if not last:
                        copy_rows(c + 1, i + 1)
                    act.wait_ge(product_done, c + 1)
                    nc.scalar.activation(partial[:, i, 0], product_ps[:, i, 0:P], ACT.Copy,
                                         scale=coef(c, 0)).then_inc(part0_done, 1)

            copy_rows(0, 0)
            each(act, body, B, RING)

        @block.vector
        def _(dve):
            nc.vector.memset(messages[:], 0.0).then_inc(cleared, 1)
            dve.wait_ge(cleared, 1)

            def add_part(at, i, r, out):
                return nc.vector.scalar_tensor_tensor(
                    out=out, in0=product_ps[:, i, r * P:(r + 1) * P], scalar=coef(at.b * CPB + i, r),
                    in1=partial[:, i, r - 1], op0=ALU.mult, op1=ALU.add)

            def body(at):
                for i in range(0, CPB, 2):
                    c = at.b * CPB + i
                    dve.wait_ge(part0_done, c + 2)
                    if at.at_least(1):
                        dve.sem_inc(k.passed, 1)
                    for j in range(2):
                        add_part(at, i + j, 1, partial[:, i + j, 1]).then_inc(added, 1)
                    for j in range(2):
                        dve.wait_ge(added, 2 * c + 1 + j)
                        add_part(at, i + j, 2, partial[:, i + j, 2]).then_inc(added, 1)
                    if i == 0:
                        if at.at_least(RING):
                            dve.wait_ge(stored[at.slot], at.turn * 16)
                        nc.vector.tensor_copy(messages[:, at.slot, :, P],
                                              k.dst_col[:, bass.ds(at.b * CPB, CPB)]).then_inc(marked, 1)
                    for j in range(2):
                        dve.wait_ge(added, 2 * c + 3 + j)
                        add_part(at, i + j, 3, messages[:, at.slot, i + j, 0:P]).then_inc(message_done, 1)

            each(dve, body, B, RING)

        @block.sync
        def _(sp):
            def body(at):
                sp.wait_ge(marked, at.b + 1)
                sp.sem_inc(k.passed, 1)
                sp.wait_ge(message_done, (at.b + 1) * CPB)
                sp.sem_inc(k.passed, 1)
                sp.dma_start(block_rows(dram, s, at),
                             messages[:, at.slot].rearrange("p c r -> p (c r)")).then_inc(stored[at.slot], 16)

            each(sp, body, B, RING)
            for slot in range(RING):
                sp.wait_ge(stored[slot], 16 * len(range(slot, B, RING)))


def conv_phase(nc, s, k, dram, layer, table, out):
    name = f"c{layer}"
    normed = layer == 1
    with ExitStack() as ctx:
        sem = ctx.enter_context(phase_semaphores(nc, f"{name}_"))
        sums = Sums(nc, ctx, sem, s, k, dram, name, False)
        norm = Norm(nc, ctx, sem, name) if normed else None
        sb = lambda n, sh, dt=FP32: ctx.enter_context(nc.sbuf_tensor(f"{name}_{n}", sh, dt))
        ps = lambda n: ctx.enter_context(nc.psum_tensor(f"{name}_{n}", [P, TPB, P], FP32))
        rows = sb("rows", [P, UNROLL, TPB, P])
        residual = sb("residual", [P, UNROLL, TPB, P]) if normed else None
        rows_t = sb("rows_t", [P, 4, TPB, P])
        biased = None if normed else sb("biased", [P, 2, TPB, P])
        relu = None if normed else sb("relu", [P, UNROLL, TPB, P])
        rows_t_ps = [ps(f"rows_t_ps{i}") for i in range(2)]
        sums_ps = [ps(f"sums{i}") for i in range(2)]
        rows_loaded = [sem(f"rows_loaded{i}") for i in range(UNROLL // PAIR)]
        residual_loaded = [sem(f"residual_loaded{i}") for i in range(UNROLL // PAIR)]
        stored = [sem(f"stored{i}") for i in range(UNROLL // PAIR)]
        turned = sem("rows_turned")
        rows_t_done = sem("rows_t_copied")
        own_done = sem("own_product_done")
        relu_done = sem("relu_done")
        bias_added = sem("bias_added")
        B = s.batches
        block = ctx.enter_context(nc.Block())
        finished = (lambda b: (norm.summed, b + 1)) if normed else (lambda b: (bias_added, b + 1))

        @block.sync
        def _(sp):
            def load_rows(at):
                if at.at_least(UNROLL):
                    sp.wait_ge(turned, at.b - UNROLL + PAIR)
                    sp.sem_inc(k.passed, 1)
                load_pair(sp, s, k, table, at, rows, rows_loaded, None)

            def body(at):
                if at.slot % PAIR == 0:
                    if at.ahead(PAIR).within(B):
                        load_rows(at.ahead(PAIR))
                    if normed:
                        if at.at_least(UNROLL):
                            sp.wait_ge(norm.summed, at.b - UNROLL + PAIR)
                            sp.sem_inc(k.passed, 1)
                        load_pair(sp, s, k, dram.x1, at, residual, residual_loaded, None)
                sums.load(sp, at, None)

            load_rows(At(0, 0, 0, UNROLL))
            each(sp, body, B, UNROLL)

        @block.vector
        def _(dve):
            if normed:
                norm.constants()
            sums.begin(dve)

            def body(at):
                prev, two, three = at.back(1), at.back(2), at.back(3)
                if at.within(B):
                    sums.build_steps(dve, at)
                    sums.build(dve, at)
                if normed and two.within(B):
                    norm.aggregate(dve, two)
                if not normed:
                    if prev.within(B):
                        dve.wait_ge(sums.added, prev.b + 1)
                        if prev.at_least(2):
                            dve.wait_ge(relu_done, prev.b - 1)
                        nc.vector.tensor_tensor(biased[:, prev.slot % 2], sums_ps[prev.slot % 2][:], k.bias_rows[:],
                                                ALU.add).then_inc(bias_added, 1)
                    return
                if three.within(B):
                    norm.invert(dve, three)
                if prev.within(B):
                    dve.wait_ge(sums.added, prev.b + 1)
                    dve.wait_ge(residual_loaded[prev.slot // PAIR], (prev.turn + 1) * 16)
                    norm.sum(dve, prev, sums_ps[prev.slot % 2][:], residual[:, prev.slot])
                if three.within(B):
                    norm.offset(dve, three)
                if prev.within(B):
                    norm.statistics(dve, prev)

            each(dve, body, B, UNROLL, drain=3 if normed else 1)

        @block.tensor
        def _(pe):
            def turn(at):
                pe.wait_ge(rows_loaded[at.slot // PAIR], (at.turn + 1) * 16)
                if at.at_least(2):
                    pe.wait_ge(rows_t_done, at.b - 1)
                for j in range(TPB):
                    last = nc.tensor.transpose(rows_t_ps[at.slot % 2][:, j], rows[:, at.slot, j], k.ident[:])
                last.then_inc(turned, 1)

            def body(at):
                bank = sums_ps[at.slot % 2]
                if at.at_least(2):
                    sem_, n = finished(at.b - 2)
                    pe.wait_ge(sem_, n)
                if normed:
                    nc.tensor.matmul(bank[:].rearrange("p t f -> p (t f)"), k.ones3[:], k.bias_parts[:], start=True,
                                     stop=True, skip_group_check=True)
                pe.wait_ge(rows_t_done, at.b + 1)
                for j in range(TPB):
                    last = nc.tensor.matmul(bank[:, j], rows_t[:, at.slot % 4, j], k.root[layer][:],
                                            start=(j == 0 and not normed), stop=True, skip_group_check=True)
                last.then_inc(own_done, 1)
                if at.ahead(2).within(B):
                    turn(at.ahead(2))
                sums.add_steps(pe, at, bank)
                sums.add_windows(pe, at, bank)

            for b in range(2):
                turn(At(b, b, 0, UNROLL))
            each(pe, body, B, UNROLL)

        @block.scalar
        def _(act):
            if normed:
                act.wait_ge(norm.eps_made, 1)

            def copy_rows(at):
                act.wait_ge(turned, at.b + 1)
                if at.at_least(4):
                    act.wait_ge(own_done, at.b - 3)
                nc.scalar.copy(rows_t[:, at.slot % 4], rows_t_ps[at.slot % 2][:]).then_inc(rows_t_done, 1)

            def body(at):
                if at.ahead(1).within(B):
                    copy_rows(at.ahead(1))
                prev, two, three = at.back(1), at.back(2), at.back(3)
                if normed and two.within(B):
                    norm.deviation(act, two)
                if normed and three.within(B):
                    norm.apply(act, three, stored)
                if not normed and prev.within(B):
                    act.wait_ge(bias_added, prev.b + 1)
                    if prev.at_least(UNROLL):
                        act.wait_ge(stored[prev.slot // PAIR], prev.turn * 16)
                    nc.scalar.activation(relu[:, prev.slot], biased[:, prev.slot % 2], ACT.Relu).then_inc(relu_done, 1)
                done = at.back(lag)
                if done.within(B) and done.slot % PAIR == 0:
                    if normed:
                        act.wait_ge(norm.normed, (done.b + PAIR) * TPB)
                    else:
                        act.wait_ge(relu_done, done.b + PAIR)
                    act.sem_inc(k.passed, 1)
                    store_pair(act, s, out, done, norm.out if normed else relu, stored, not normed)

            lag = 6 if normed else 4
            copy_rows(At(0, 0, 0, UNROLL))
            each(act, body, B, UNROLL, drain=lag - PAIR + 1)
            wait_stored(act, s, stored, not normed)


class Named:
    pass


def build_program(nc, x, src, dst, edge_type, weight, w0, w1, root1, b1, w2, root2, b2, out):
    s = Shapes(x.shape[0], src.shape[0])
    dram = Named()
    dram.x, dram.src, dram.dst, dram.type, dram.w, dram.w0 = x, src, dst, edge_type, weight, w0
    dram.w1, dram.root1, dram.b1, dram.w2, dram.root2, dram.b2, dram.out = w1, root1, b1, w2, root2, b2, out
    rows = s.batches * TPB * P
    dram.x1 = nc.dram_tensor("x1_rows", (rows, P), FP32).ap()
    dram.h1 = nc.dram_tensor("h1_rows", (rows, P), FP32).ap()
    dram.edge_rows = nc.dram_tensor("edge_rows", (s.rows, ROW), FP32).ap()
    dram.starts = nc.dram_tensor("tile_starts", (1, DIGIT * DIGIT), FP32).ap()
    with ExitStack() as ctx:
        k = Named()
        sb = lambda n, sh, dt=FP32: ctx.enter_context(nc.sbuf_tensor(n, sh, dt))
        k.node = sb("node_numbers", [P, TPB * P])
        k.minus_base = sb("minus_batch_base", [P, s.batches])
        k.ident = sb("identity", [P, P])
        k.zeros = sb("zeros", [P, TPB * P])
        k.ones3 = sb("ones3", [3, P], BF16)
        k.dst_col = sb("dst_col", [P, s.blocks * CPB])
        k.src_col = sb("src_col", [P, s.blocks * CPB], I32)
        k.coef = sb("coef", [P, s.blocks * CPB * RELATIONS])
        k.kind = sb("batch_kind", [1, s.batches + KINDS], I32)
        k.table = sb("batch_table", [1, s.batches * 4], I32)
        k.w0t = sb("w0t", [P, P])
        k.root = [sb(f"root{i}", [P, P]) for i in range(2)]
        k.wrel = [sb(f"wrel{i}", [P, RELATIONS * P]) for i in range(2)]
        k.bias_rows = sb("bias_rows", [P, TPB, P])
        k.bias_parts = sb("bias_parts", [3, TPB * P], BF16)
        k.gathered = [ctx.enter_context(nc.semaphore(f"gathered{i}")) for i in range(RING)]
        k.rows_stored = [ctx.enter_context(nc.semaphore(f"rows_stored{i}")) for i in range(RING)]
        k.index = sb("l0_index", [P, RING, CPB], I32)
        k.gather_ring = sb("gather_ring", [P, RING, CPB, ROW])
        k.staged = ctx.enter_context(nc.semaphore("l0_index_staged"))
        k.marked = ctx.enter_context(nc.semaphore("l0_marked"))
        k.blocks_stored = ctx.enter_context(nc.semaphore("l0_blocks_stored"))
        k.passed = ctx.enter_context(nc.semaphore("waits_passed"))
        setup_phase(nc, s, k, dram)
        first_phase(nc, s, k, dram)
        message_phase(nc, s, k, dram, 0, dram.x1)
        conv_phase(nc, s, k, dram, 0, dram.x1, dram.h1)
        message_phase(nc, s, k, dram, 1, dram.h1)
        conv_phase(nc, s, k, dram, 1, dram.h1, dram.out)


_INS = ['x', 'src', 'dst', 'edge_type_4', 'edge_weight', 'L0_gnn_W', 'L1_gnn_W1', 'L1_gnn_root1', 'L1_gnn_b1',
        'L1_gnn_W2', 'L1_gnn_root2', 'L1_gnn_b2']


def kernel(**inputs):
    import numpy as _np
    import concourse.bacc as _bacc
    from concourse import mybir as _mybir
    from concourse.bass_utils import run_bass_kernel_spmd as _run

    nc = _bacc.Bacc("TRN2", target_bir_lowering=False, num_devices=1)
    arrays, args = {}, []
    for name in _INS:
        a = _np.ascontiguousarray(inputs[name])
        arrays[f"in_{name}"] = a
        args.append(nc.dram_tensor(f"in_{name}", a.shape, _mybir.dt.from_np(a.dtype), kind="ExternalInput").ap())
    shape = inputs['x'].shape
    args.append(nc.dram_tensor("out_rows", tuple(shape), FP32, kind="ExternalOutput").ap())
    build_program(nc, *args)
    r = _run(nc, [arrays], core_ids=[0])
    return r.results[0]["out_rows"]
```
